# Optimizing a Trainium2 kernel written in Bass

```python
import numpy as np
import jax
import jax.numpy as jnp

def _softmax(x, axis=-1):
    return jax.nn.softmax(x, axis=axis)

def _gelu(x):
    return jax.nn.gelu(x, approximate=True)

def _silu(x):
    return jax.nn.silu(x)

def _sigmoid(x):
    return jax.nn.sigmoid(x)

def _layernorm(x, axis=-1, eps=1e-05):
    m = jnp.mean(x, axis=axis, keepdims=True)
    v = jnp.var(x, axis=axis, keepdims=True)
    return (x - m) / jnp.sqrt(v + eps)

def _scatter_add(tgt, idx, src, axis=0):
    return tgt.at[idx].add(src)

def _segment_sum(src, seg, n):
    return jax.ops.segment_sum(src, seg, n)
kernel_name = 'mk_xattn_ffn_d1_seqx_r8_0c244f'

def setup_inputs(seed: int=0):
    np.random.seed(seed)
    _w = jnp.asarray

    def _rec_inputs():
        import jax
        import jax.numpy as jnp
        _rk = jax.random.key(seed)
        x = -0.0002928 + 1 * jax.random.normal(jax.random.fold_in(_rk, 1), (4, 256, 128), jnp.float32)
        _lenS = 256 - jax.random.randint(jax.random.fold_in(_rk, 7), (4,), 0, max(1, 256 // 4) + 1, jnp.int32)
        _lenS2 = 64 - jax.random.randint(jax.random.fold_in(_rk, 8), (4,), 0, max(1, 64 // 4) + 1, jnp.int32)
        _ctx_1024P = jax.random.normal(jax.random.fold_in(_rk, 11), (4, 16, 128), jnp.float32)
        _ctx_1024c = jax.random.dirichlet(jax.random.fold_in(_rk, 511), 0.3 * jnp.ones((16,), jnp.float32), (4, 64))
        _ctx_1024t = jnp.einsum('bsk,bkd->bsd', _ctx_1024c, _ctx_1024P)
        _ctx_1024t = _ctx_1024t * jax.lax.rsqrt(jnp.mean(jnp.square(_ctx_1024t)) + 1e-12) * 0.953939
        ctx_1024 = -1.39393e-06 + 0.999914 * (_ctx_1024t + 0.3 * jax.random.normal(jax.random.fold_in(_rk, 611), (4, 64, 128), jnp.float32))
        _validS = jnp.arange(256)[None, :] < _lenS[:, None]
        _validS2 = jnp.arange(64)[None, :] < _lenS2[:, None]
        _causal = jnp.tril(jnp.ones((256, 256), dtype=bool))
        mask_BxS2_bk0 = jnp.logical_not(jnp.broadcast_to(_validS2[:, :], (4, 64)))
        return (x, ctx_1024, mask_BxS2_bk0)
    x, ctx_1024, mask_BxS2_bk0 = _rec_inputs()

    def _L0_xattn_setup():
        import jax, jax.numpy as jnp
        import numpy as np
        B, TQ, TK, D, H = (2, 256, 256, 128, 16)
        HD = D // H
        NUM_PAD = 32
        key = jax.random.key(seed)
        ks = jax.random.split(key, 8)
        s = 0.02
        q = jax.random.normal(ks[0], (B, TQ, D), dtype=jnp.float32)
        kv = jax.random.normal(ks[1], (B, TK, D), dtype=jnp.float32)
        key_padding_mask = jnp.broadcast_to(jnp.arange(TK) >= TK - NUM_PAD, (B, TK))
        Wq = jax.random.normal(ks[2], (D, D), dtype=jnp.float32) * s
        bq = jax.random.normal(ks[3], (D,), dtype=jnp.float32) * s
        Wkv = jax.random.normal(ks[4], (D, 2 * D), dtype=jnp.float32) * s
        bkv = jax.random.normal(ks[5], (2 * D,), dtype=jnp.float32) * s
        Wo = jax.random.normal(ks[6], (D, D), dtype=jnp.float32) * s
        bo = jax.random.normal(ks[7], (D,), dtype=jnp.float32) * s
        return {'q': q, 'kv': kv, 'key_padding_mask': key_padding_mask, 'Wq': Wq, 'bq': bq, 'Wkv': Wkv, 'bkv': bkv, 'Wo': Wo, 'bo': bo}
    _L0_xattn_all = _L0_xattn_setup()
    _L0_xattn_in = {k: v for k, v in _L0_xattn_all.items() if k in ('Wq', 'bq', 'Wkv', 'bkv', 'Wo', 'bo')}
    del _L0_xattn_all

    def _L0_ffn_setup():
        import jax, jax.numpy as jnp
        import numpy as np
        B, S, F, E, K = (4, 128, 128, 8, 2)
        H = 4 * F
        key = jax.random.key(seed)
        ks = jax.random.split(key, 7)

        def xavier(k, shape):
            fan_in, fan_out = (shape[-2], shape[-1])
            scale = jnp.sqrt(6.0 / (fan_in + fan_out))
            return jax.random.uniform(k, shape, jnp.float32, -scale, scale)
        return {'x': jax.random.normal(ks[0], (B, S, F), jnp.float32), 'Wg': xavier(ks[1], (F, E)), 'bg': jnp.zeros((E,), jnp.float32), 'W1': xavier(ks[2], (E, F, H)), 'b1': jnp.zeros((E, H), jnp.float32), 'W2': xavier(ks[3], (E, H, F)), 'b2': jnp.zeros((E, F), jnp.float32)}
    _L0_ffn_all = _L0_ffn_setup()
    _L0_ffn_in = {k: v for k, v in _L0_ffn_all.items() if k in ('Wg', 'bg', 'W1', 'b1', 'W2', 'b2')}
    del _L0_ffn_all
    return {'x': x, 'ctx_1024': ctx_1024, 'mask_BxS2_bk0': mask_BxS2_bk0, 'L0_xattn_Wq': _L0_xattn_in['Wq'], 'L0_xattn_bq': _L0_xattn_in['bq'], 'L0_xattn_Wkv': _L0_xattn_in['Wkv'], 'L0_xattn_bkv': _L0_xattn_in['bkv'], 'L0_xattn_Wo': _L0_xattn_in['Wo'], 'L0_xattn_bo': _L0_xattn_in['bo'], 'L0_ffn_Wg': _L0_ffn_in['Wg'], 'L0_ffn_bg': _L0_ffn_in['bg'], 'L0_ffn_W1': _L0_ffn_in['W1'], 'L0_ffn_b1': _L0_ffn_in['b1'], 'L0_ffn_W2': _L0_ffn_in['W2'], 'L0_ffn_b2': _L0_ffn_in['b2']}

def reference(x, ctx_1024, mask_BxS2_bk0, L0_xattn_Wq, L0_xattn_bq, L0_xattn_Wkv, L0_xattn_bkv, L0_xattn_Wo, L0_xattn_bo, L0_ffn_Wg, L0_ffn_bg, L0_ffn_W1, L0_ffn_b1, L0_ffn_W2, L0_ffn_b2):
    import jax
    import jax.numpy as jnp

    def _L0_xattn_ref(q, kv, key_padding_mask, Wq, bq, Wkv, bkv, Wo, bo):
        import jax, jax.numpy as jnp
        import numpy as np
        B, TQ, TK, D, H = (2, 256, 256, 128, 16)
        HD = D // H
        NUM_PAD = 32
        Bc, Tq, Dm = q.shape
        Tk = kv.shape[1]
        scale = HD ** (-0.5)
        Q = (q @ Wq + bq).reshape(Bc, Tq, H, HD).transpose(0, 2, 1, 3)
        KV = (kv @ Wkv + bkv).reshape(Bc, Tk, 2, H, HD).transpose(2, 0, 3, 1, 4)
        K, V = (KV[0], KV[1])
        attn = jnp.einsum('bhqd,bhkd->bhqk', Q, K) * scale
        attn = jnp.where(key_padding_mask[:, None, None, :], -jnp.inf, attn)
        attn = jax.nn.softmax(attn, axis=-1)
        out = jnp.einsum('bhqk,bhkd->bhqd', attn, V)
        out = out.transpose(0, 2, 1, 3).reshape(Bc, Tq, Dm)
        return out @ Wo + bo

    def _L0_ffn_ref(x, Wg, bg, W1, b1, W2, b2):
        import jax, jax.numpy as jnp
        import numpy as np
        B, S, F, E, K = (4, 128, 128, 8, 2)
        H = 4 * F
        gate_probs = jax.nn.softmax(x @ Wg + bg, axis=-1)
        k = K
        _, top_idx = jax.lax.top_k(gate_probs, k)
        expert_mask = jax.nn.one_hot(top_idx, gate_probs.shape[-1], dtype=gate_probs.dtype).sum(-2)
        selected = gate_probs * expert_mask
        selected = selected / (selected.sum(-1, keepdims=True) + 1e-08)
        h = jax.nn.gelu(jnp.einsum('bsf,efh->bseh', x, W1) + b1)
        expert_out = jnp.einsum('bseh,ehf->bsef', h, W2) + b2[None, None]
        return jnp.einsum('bsef,bse->bsf', expert_out, selected)
    x = x + _L0_xattn_ref(_layernorm(x, axis=-1), ctx_1024, mask_BxS2_bk0, L0_xattn_Wq, L0_xattn_bq, L0_xattn_Wkv, L0_xattn_bkv, L0_xattn_Wo, L0_xattn_bo)
    x = x + _L0_ffn_ref(_layernorm(x, axis=-1), L0_ffn_Wg, L0_ffn_bg, L0_ffn_W1, L0_ffn_b1, L0_ffn_W2, L0_ffn_b2)
    return x

_drawn_inputs = setup_inputs


def setup_inputs(seed=0):
    import zlib

    import numpy as np

    out = dict(_drawn_inputs(seed))
    spreads = {'L0_ffn_bg': (0.0, 0.1), 'L0_ffn_b1': (0.0, 0.1), 'L0_ffn_b2': (0.0, 0.1)}
    factors = {'L0_xattn_Wq': 29.052, 'L0_xattn_bq': 200.0, 'L0_xattn_bkv': 5.775}
    for name, (base, spread) in spreads.items():
        noise = np.random.default_rng([zlib.crc32(name.encode()), seed]).standard_normal(out[name].shape)
        drawn = base * np.exp(spread * noise) if base else spread * noise
        out[name] = jnp.asarray(drawn.astype(out[name].dtype))
    for name, factor in factors.items():
        out[name] = (out[name] * factor).astype(out[name].dtype)
    return out
```

```python
from contextlib import ExitStack

import concourse.bass as bass
from concourse import mybir

F32 = mybir.dt.float32
F32R = mybir.dt.float32r
U8 = mybir.dt.uint8
I32 = mybir.dt.int32
U32 = mybir.dt.uint32
ALU = mybir.AluOpType
ACT = mybir.ActivationFunctionType
AX = mybir.AxisListType

P = 128
EPS = 1e-5
MASKED = -1e30
HEADS = 16


def build(nc, x, ctx_in, mask, Wq, bq, Wkv, bkv, Wo, bo, Wg, bg, W1, b1, W2, b2, out):
    B, S, D = x.shape
    SK = ctx_in.shape[1]
    E, _, HID = W1.shape
    T = B * S // P
    TB = S // P
    NH = 2
    TH = T // NH
    HT = TH * P
    BH = B // NH
    HC = HID // P
    HD = D // HEADS
    SCALE = float(HD) ** -0.5
    G = 4
    GH = HEADS // G
    PR = HEADS // 2
    KEYS = B * SK
    EXT = 96
    VW = 2 * HD + 2
    assert D == P and GH * HD == 32 and 2 * SK == P and TB == 2 and HT == 512 and KEYS == 256

    with ExitStack() as stack:
        def sb(name, shape, dt=F32):
            return stack.enter_context(nc.sbuf_tensor(name, shape, dt))

        def sem(name):
            return stack.enter_context(nc.semaphore(name))

        bank = [stack.enter_context(nc.psum_tensor(f"bank{i}", [P, 512], F32)) for i in range(8)]

        x_sb = sb("x_sb", [P, T, D])
        ctx_sb = sb("ctx_sb", [P, KEYS // P, D])
        wq_sb = sb("wq_sb", [P, D])
        wkv_sb = sb("wkv_sb", [P, 2 * D])
        wo_sb = sb("wo_sb", [P, D])
        wg_sb = sb("wg_sb", [P, E])
        w1_sb = sb("w1_sb", [P, E, HID])
        w2_sb = sb("w2_sb", [P, E, HC * D])
        NB1 = E * HC
        R2, RQ, RK, NR = NB1, NB1 + E, NB1 + E + G, NB1 + E + 2 * G
        bias_rows = sb("bias_rows", [NR, P])
        bias_cols = sb("bias_cols", [P, NR])
        bv_bc = sb("bv_bc", [P, D])
        bo_bc = sb("bo_bc", [P, D])
        bg_bc = sb("bg_bc", [P, E])
        mask_row = sb("mask_row", [P, KEYS], U8)

        mask_add = sb("mask_add", [P, KEYS])

        ident = sb("ident", [P, P])
        part_i = sb("part_i", [P, GH], I32)
        head_of = sb("head_of", [P, GH], I32)
        col_j = sb("col_j", [P, GH], I32)
        own_head = sb("own_head", [P, GH])
        minus_half = sb("minus_half", [P, T])
        col_e = sb("col_e", [P, E], I32)
        pick = sb("pick", [2 * E, E, P])
        pick_r = sb("pick_r", [2 * E, E, P], F32R)

        wq_rep = sb("wq_rep", [P, G, 3, 32])
        wk_rep = sb("wk_rep", [P, G, 3, 32])
        ctxT = sb("ctxT", [P, B, 2, SK])
        k_mix = sb("k_mix", [EXT, G, KEYS], F32R)
        k_blk = sb("k_blk", [P, G, B, GH, SK], F32R)
        v_blk = sb("v_blk", [P, B, PR, VW])
        stats = sb("stats", [P, T, 6])
        mv1 = sb("mv1", [P, T, 2])
        rstd1 = sb("rstd1", [P, T])
        xn = sb("xn", [P, T, D])
        xnT = sb("xnT", [P, NH, HT])
        q_st = sb("q_st", [P, G, T * P], F32R)
        nmax = sb("nmax", [P, T, HEADS])
        nm_cols = sb("nm_cols", [P, T, G, 32], F32R)
        probs_mem = sb("probs_mem", [P, 2 * PR * S])
        probsT = probs_mem[:].rearrange("p (r a q) -> p r a q", r=2, a=PR)
        ext_sel = probs_mem[:, 0:GH * KEYS].rearrange("p (b j k) -> p b j k", b=B, j=GH)
        rsum = sb("rsum", [P, 2, TB, HEADS])
        attn = sb("attn", [P, 2, TB, D])
        attnT = sb("attnT", [P, 2, S])
        xb = sb("xb", [P, T, D])
        x1 = sb("x1", [P, T, D])

        mv2 = sb("mv2", [P, T, 2])
        rstd2 = sb("rstd2", [P, T])
        x2n = xn
        x2T = xnT[:].rearrange("p h q -> p (h q)")
        x2T_hi = sb("x2T_hi", [P, T * P], F32R)
        x2T_lo = sb("x2T_lo", [P, T * P], F32R)
        logit = sb("logit", [P, T, E])
        lmax = sb("lmax", [P, T])
        prob = sb("prob", [P, T, E])
        psumv = sb("psumv", [P, T])
        top = sb("top", [P, T, E])
        top_at = sb("top_at", [P, T, E], U32)
        first = sb("first", [P, T, E])
        second = sb("second", [P, T, E])
        norm = sb("norm", [P, T])
        sel = sb("sel", [P, T, E])
        sel_parts = sb("sel_parts", [P, T, 2 * E], F32R)
        selT = sb("selT", [2 * E, NH, HT], F32R)
        sel_bc = sb("sel_bc", [P, E, NH, HT])

        w_hi = sb("w_hi", [P, 2, 2, HID], F32R)
        w_lo = sb("w_lo", [P, 2, 2, HID], F32R)
        RING = 4
        hid = probs_mem[:, 0:RING * HT].rearrange("p (r q) -> p r q", r=RING)
        part = probs_mem[:, RING * HT:(RING + 2) * HT].rearrange("p (r q) -> p r q", r=2)
        k_mem = k_blk[:].rearrange("p g b j k -> p (g b j k)")
        hid_hi = k_mem[:, 0:RING * HT].rearrange("p (r q) -> p r q", r=RING)
        hid_lo = k_mem[:, RING * HT:2 * RING * HT].rearrange("p (r q) -> p r q", r=RING)
        acc = sb("acc", [P, NH, HT])
        b1_now = sb("b1_now", [P, 2, HC])
        y_out = x_sb

        ld_x = [sem(f"ld_x{h}") for h in range(NH)]
        ld_ctx, ld_wq, ld_wkv, ld_wo, ld_wg = (sem(n) for n in ("ld_ctx", "ld_wq", "ld_wkv", "ld_wo", "ld_wg"))
        ld_w = [sem(f"ld_w{e}") for e in range(E)]
        ld_bias, ld_bv, ld_bo, ld_bg, ld_mask = (sem(n) for n in ("ld_bias", "ld_bv", "ld_bo", "ld_bg", "ld_mask"))
        stored = sem("stored")
        pool_step = sem("pool_step")
        zeroed = sem("zeroed")
        ident_ready = sem("ident_ready")
        index_ready = sem("index_ready")
        fill_ready = sem("fill_ready")
        pick_ready = sem("pick_ready")
        ext_ready = sem("ext_ready")
        xb_ready = sem("xb_ready")
        dve_step = sem("dve_step")
        rep_ready = sem("rep_ready")
        own_ready = sem("own_ready")
        biasT_done, bias_ready = sem("biasT_done"), sem("bias_ready")
        ctxT_done, ctxT_ready = sem("ctxT_done"), sem("ctxT_ready")
        k_done, k_hi, k_lo, k_ready = (sem(n) for n in ("k_done", "k_hi", "k_lo", "k_ready"))
        v_done, v_ready = sem("v_done"), sem("v_ready")
        var1, rstd1_ready, xn_ready = sem("var1"), sem("rstd1_ready"), sem("xn_ready")
        xnT_done, xnT_ready = sem("xnT_done"), sem("xnT_ready")
        q_done, q_hi, q_lo = sem("q_done"), sem("q_hi"), sem("q_lo")
        s_done, max_read, nm_ready = sem("s_done"), sem("max_read"), sem("nm_ready")
        nmT_done, nmT_ready = sem("nmT_done"), sem("nmT_ready")
        st_done, exp_done = sem("st_done"), sem("exp_done")
        pv_done, attn_ready = sem("pv_done"), sem("attn_ready")
        attnT_done, attnT_ready = sem("attnT_done"), sem("attnT_ready")
        proj_done, x1_ready = sem("proj_done"), sem("x1_ready")
        var2, rstd2_ready, x2n_ready = sem("var2"), sem("rstd2_ready"), sem("x2n_ready")
        x2T_done, x2T_ready, x2hi_ready, x2lo_ready = (sem(n) for n in ("x2T_done", "x2T_ready", "x2hi_ready", "x2lo_ready"))
        gate_done, logit_ready, prob_exp, sel_ready = (sem(n) for n in ("gate_done", "logit_ready", "prob_exp", "sel_ready"))
        selT_done, selT_ready, bc_done, bc_ready = (sem(n) for n in ("selT_done", "selT_ready", "bc_done", "bc_ready"))
        pick_r_ready = sem("pick_r_ready")
        acc_zero = sem("acc_zero")
        wsplit_hi = sem("wsplit_hi")
        wsplit = sem("wsplit")
        up_done, gelu_done = sem("up_done"), sem("gelu_done")
        b1_ready = sem("b1_ready")
        hid_split, lo_dve, lo_pool, down_done = (sem(n) for n in ("hid_split", "lo_dve", "lo_pool", "down_done"))
        y_scaled, y_added = sem("y_scaled"), sem("y_added")
        outT_done, out_ready = sem("outT_done"), sem("out_ready")

        x_t = x.rearrange("b (t p) d -> p (b t) d", p=P)
        out_t = out.rearrange("b (t p) d -> p (b t) d", p=P)

        block = stack.enter_context(nc.Block())

        PER = 2 * NH * HC
        ITER = E // 2
        AHEAD = RING
        known = lambda v: isinstance(v, int)

        def after(eng, s, value):
            if not known(value) or value > 0:
                eng.wait_ge(s, value)

        def wait_lo(eng, unit, hc):
            if hc == HC - 1:
                after(eng, lo_pool, unit + 1)
            else:
                after(eng, lo_dve, (HC - 1) * unit + hc + 1) if not known(unit) or unit >= 0 else None

        def hid_low(eng, jj):
            return eng.tensor_tensor(hid_lo[:, jj % RING, :], hid[:, jj % RING, :],
                                     hid_hi[:, jj % RING, :].bitcast(F32), ALU.subtract)

        def weight(e, which):
            w = (w1_sb, w2_sb)[which]
            return w[:, e, :] if known(e) else w[:, bass.ds(e, 1), :].rearrange("p a n -> p (a n)")

        def iterations(eng, body):
            body(0)
            with eng.Fori(1, ITER - 1) as i:
                body(i)
            body(ITER - 1)

        @block.sync
        def _(sp):
            for h in range(NH):
                sp.dma_start(x_sb[:, h * TH:(h + 1) * TH, :], x_t[:, h * TH:(h + 1) * TH, :]).then_inc(ld_x[h], 16)
                if h == 0:
                    sp.dma_start(wkv_sb[:], Wkv).then_inc(ld_wkv, 16)
                    sp.dma_start(wq_sb[:], Wq).then_inc(ld_wq, 16)
            sp.dma_start(wo_sb[:], Wo).then_inc(ld_wo, 16)
            sp.dma_start(wg_sb[:], Wg).then_inc(ld_wg, 16)
            sp.dma_start(bo_bc[:], bo.rearrange("(a d) -> a d", a=1).to_broadcast([P, D])).then_inc(ld_bo, 16)
            sp.dma_start(bg_bc[:], bg.rearrange("(a d) -> a d", a=1).to_broadcast([P, E])).then_inc(ld_bg, 16)
            for e in range(E):
                sp.dma_start(w1_sb[:, e, :], W1[e]).then_inc(ld_w[e], 16)
                sp.dma_start(w2_sb[:, e, :].rearrange("p (c f) -> p c f", c=HC),
                             W2[e].rearrange("(c p) f -> p c f", p=P)).then_inc(ld_w[e], 16)
            for h in range(NH):
                sp.wait_ge(out_ready, h + 1)
                sp.dma_start(out_t[:, h * TH:(h + 1) * TH, :], y_out[:, h * TH:(h + 1) * TH, :]).then_inc(stored, 16)
            sp.wait_ge(stored, 16 * NH)

        @block.gpsimd
        def _(pool):
            steps = [0]

            def link(ins):
                steps[0] += 1
                ins.then_inc(pool_step, 1)
                pool.wait_ge(pool_step, steps[0])

            pool.memset(bias_rows[:], 0.0).then_inc(zeroed, 1)
            pool.wait_ge(zeroed, 1)
            pool.memset(mask_row[EXT:P, :], 0).then_inc(zeroed, 1)
            pool.wait_ge(zeroed, 2)
            link(pool.memset(ident[:], 0.0))
            pool.affine_select(out=ident[:], in_=ident[:], compare_op=ALU.not_equal, fill=1.0, base=0,
                               pattern=[[-1, P]], channel_multiplier=1).then_inc(ident_ready, 1)
            pool.memset(minus_half[:], -0.5)
            pool.iota(part_i[:], pattern=[[0, GH]], base=0, channel_multiplier=1).then_inc(index_ready, 1)
            pool.iota(col_j[:], pattern=[[1, GH]], base=0, channel_multiplier=0).then_inc(index_ready, 1)
            pool.iota(col_e[:], pattern=[[1, E]], base=0, channel_multiplier=0).then_inc(index_ready, 1)
            pool.wait_ge(index_ready, 3)

            def rstd(mv, rs, lo, hi):
                link(pool.tensor_scalar(rs[:, lo:hi], mv[:, lo:hi, 1], EPS, 1.0, ALU.add, ALU.mult))
                return pool.tensor_tensor(rs[:, lo:hi], rs[:, lo:hi], minus_half[:, lo:hi], ALU.pow)

            ext = ext_sel[EXT:P, :, :, :]
            link(pool.memset(ext, 0.0))
            for first_row in (1, 1 + GH):
                link(pool.affine_select(out=ext, in_=ext, compare_op=ALU.not_equal, fill=1.0, base=-first_row,
                                        pattern=[[0, B], [-1, GH], [0, SK]], channel_multiplier=1))
            pool.wait_ge(var1, 1)
            rstd(mv1, rstd1, 0, TH).then_inc(rstd1_ready, 1)
            pool.wait_ge(rstd1_ready, 1)
            link(pool.memset(q_st[EXT:P, :, :].bitcast(F32), 0.0))
            pool.memset(q_st[EXT:EXT + 1, :, :].bitcast(F32), 1.0).then_inc(fill_ready, 1)
            pool.wait_ge(fill_ready, 1)
            pool.wait_ge(ld_mask, 16)
            link(pool.tensor_scalar(mask_add[EXT:P, :], mask_row[EXT:P, :], MASKED, 1.0, ALU.mult, ALU.mult))
            for g in range(2):
                pool.tensor_tensor(k_blk[EXT:P, g, :, :, :], ext, mask_add[EXT:P, :].rearrange("p (b k) -> p b k", b=B)
                                   .unsqueeze(2).to_broadcast([P - EXT, B, GH, SK]),
                                   ALU.add).then_inc(ext_ready, 1)
                pool.wait_ge(ext_ready, g + 1)
            link(pool.memset(nm_cols[:].bitcast(F32), 0.0))
            pool.memset(nm_cols[:, :, :, 0:1].bitcast(F32), 1.0).then_inc(fill_ready, 1)
            pool.wait_ge(var1, 2)
            rstd(mv1, rstd1, TH, T).then_inc(rstd1_ready, 1)
            link(pool.memset(v_blk[:], 0.0))
            pool.memset(v_blk[0:SK, :, :, 2 * HD:2 * HD + 1], 1.0).then_inc(fill_ready, 1)
            pool.wait_ge(fill_ready, 3)
            pool.memset(v_blk[SK:P, :, :, 2 * HD + 1:VW], 1.0).then_inc(fill_ready, 1)
            pool.wait_ge(fill_ready, 4)
            pool.wait_ge(ld_bo, 16)
            for h in range(NH):
                pool.wait_ge(ld_x[h], 16)
                t = slice(h * TH, (h + 1) * TH)
                pool.tensor_tensor(xb[:, t, :], x_sb[:, t, :],
                                   bo_bc[:].unsqueeze(1).to_broadcast([P, TH, D]), ALU.add).then_inc(xb_ready, 1)

            def weight_lo(e, slot, which):
                pool.wait_ge(wsplit_hi, 2 * e + which + 1)
                pool.tensor_tensor(w_lo[:, slot, which, :], weight(e, which), w_hi[:, slot, which, :].bitcast(F32),
                                   ALU.subtract).then_inc(wsplit, 1)

            link(pool.memset(pick[:], 0.0))
            for first_row in (0, E):
                ins = pool.affine_select(out=pick[:], in_=pick[:], compare_op=ALU.not_equal, fill=1.0,
                                         base=-first_row, pattern=[[-1, E], [0, P]], channel_multiplier=1)
                if first_row == 0:
                    link(ins)
            ins.then_inc(pick_ready, 1)
            pool.memset(acc[:], 0.0).then_inc(acc_zero, 1)
            for b in range(B):
                if b < 2:
                    pool.wait_ge(ld_w[b], 32)
                    for which in range(2):
                        pool.tensor_scalar(w_hi[:, b, which, :], weight(b, which), 1.0, 1.0, ALU.mult, ALU.mult).then_inc(wsplit_hi, 1)
                        weight_lo(b, b, which)
                pool.wait_ge(var2, b + 1)
                rstd(mv2, rstd2, TB * b, TB * (b + 1)).then_inc(rstd2_ready, 1)
            for e in range(2, E):
                pool.wait_ge(ld_w[e], 32)
            pool.wait_ge(acc_zero, 1)

            def body(i):
                for jj in range(PER):
                    j = i * PER + jj
                    slot = jj // (2 * HC)
                    if jj % HC == HC - 1:
                        pool.wait_ge(hid_split, j + 1)
                        hid_low(pool, jj).then_inc(lo_pool, 1)
                    e = 2 * i + slot + 1
                    if jj % (2 * HC) in (4, 6) and not (known(i) and not 2 <= e < E):
                        weight_lo(e, 1 - slot, jj % (2 * HC) // 2 - 2)
                    if jj % HC == 1:
                        unit = 2 * NH * i + jj // HC - 2
                        if not known(unit) or unit >= 0:
                            add(unit, jj // HC % 2)

            def add(unit, c):
                pool.wait_ge(y_scaled, unit + 1)
                after(pool, y_added, unit - 1)
                pool.tensor_tensor(acc[:, c, :], acc[:, c, :], part[:, c, :], ALU.add).then_inc(y_added, 1)

            iterations(pool, body)
            for c in range(NH):
                add(NH * (E - 1) + c, c)

        @block.scalar
        def _(act):
            act.dma_start(ctx_sb[:], ctx_in.rearrange("b k d -> (b k) d").rearrange("(t p) d -> p t d", p=P)).then_inc(ld_ctx, 16)
            act.wait_ge(zeroed, 2)
            act.dma_start(bias_rows[0:NB1, :], b1.rearrange("e (c p) -> (e c) p", p=P)).then_inc(ld_bias, 16)
            act.dma_start(bias_rows[R2:R2 + E, :], b2).then_inc(ld_bias, 16)
            for r, b_in in ((RQ, bq), (RK, bkv[0:D])):
                for q in range(3):
                    act.dma_start(bias_rows[r:r + G, 32 * q:32 * q + 32],
                                  b_in.rearrange("(g c) -> g c", g=G)).then_inc(ld_bias, 16)
            act.dma_start(mask_row[EXT:EXT + 1, :],
                          mask.rearrange("(a b) k -> a (b k)", a=1)).then_inc(ld_mask, 16)
            act.dma_start(bv_bc[:], bkv[D:2 * D].rearrange("(a d) -> a d", a=1).to_broadcast([P, D])).then_inc(ld_bv, 16)

            act.wait_ge(ctxT_done, 1)
            for c in range(2):
                act.copy(ctxT[:, :, c, :], bank[6][:, 0:KEYS].rearrange("p (b k) -> p b k", b=B)).then_inc(ctxT_ready, 1)
            act.wait_ge(biasT_done, 1)
            act.copy(bias_cols[:], bank[7][:, 0:NR]).then_inc(bias_ready, 1)
            act.wait_ge(bias_ready, 1)
            for g in range(G):
                act.wait_ge(k_done, g + 1)
                act.activation(k_mix[:, g, :], bank[g][0:EXT, 0:KEYS], ACT.Identity,
                               bias=bias_cols[0:EXT, RK + g:RK + g + 1]).then_inc(k_hi, 1)

            def q_hi_of(h):
                act.wait_ge(xnT_done, h + 1)
                act.copy(xnT[:, h, :], bank[7 - h][:]).then_inc(xnT_ready, 1)
                for g in range(G):
                    n = G * h + g
                    act.wait_ge(q_done, n + 1)
                    act.activation(q_st[0:EXT, g, h * HT:(h + 1) * HT], bank[n % 4][0:EXT, :], ACT.Identity,
                                   bias=bias_cols[0:EXT, RQ + g:RQ + g + 1]).then_inc(q_hi, 1)

            def nm_rows(b):
                act.wait_ge(nmT_done, b + 1)
                for g in range(2, G):
                    act.copy(q_st[EXT:P, g, b * S:(b + 1) * S], bank[5][32 * g:32 * g + 32, 0:S]).then_inc(nmT_ready, 1)

            def exps(b):
                for n in range(PR // 2):
                    act.wait_ge(st_done, PR // 2 * b + n + 1)
                    if b >= 2 and n == 0:
                        act.wait_ge(pv_done, b - 1)
                    act.activation(probsT[:, b % 2, 2 * n:2 * n + 2, :], bank[2 + n % 2][:].rearrange("p (a q) -> p a q", a=2),
                                   ACT.Exp, scale=SCALE).then_inc(exp_done, 1)

            def attnT_of(b):
                act.wait_ge(attnT_done, b + 1)
                act.copy(attnT[:, b % 2, :], bank[4][:, 0:S]).then_inc(attnT_ready, 1)

            def x2T_of(b):
                act.wait_ge(x2T_done, b + 1)
                act.copy(x2T_hi[:, b * S:(b + 1) * S], bank[6][:, 0:S]).then_inc(x2hi_ready, 1)
                act.copy(x2T[:, b * S:(b + 1) * S], bank[6][:, 0:S]).then_inc(x2T_ready, 1)

            q_hi_of(0)
            act.wait_ge(ext_ready, 2)
            for g in range(2):
                act.copy(k_blk[EXT:P, 2 + g, :, :, :], k_blk[EXT:P, g, :, :, :].bitcast(F32)).then_inc(ext_ready, 1)
            q_hi_of(1)
            for b in range(B + 3):
                if b < B:
                    nm_rows(b)
                if 0 <= b - 1 < B:
                    attnT_of(b - 1)
                if b < B:
                    exps(b)
                if 0 <= b - 2 < B:
                    x2T_of(b - 2)
                if b - 3 in (BH - 1, B - 1):
                    h = (b - 3) // BH
                    t = slice(h * TH, (h + 1) * TH)
                    act.wait_ge(logit_ready, h + 1)
                    act.activation(prob[:, t, :], logit[:, t, :], ACT.Exp).then_inc(prob_exp, 1)
            for h in range(NH):
                act.wait_ge(selT_done, h + 1)
                act.copy(selT[:, h, :], bank[7 - h][0:2 * E, :]).then_inc(selT_ready, 1)
            for n in range(NH * E):
                act.wait_ge(bc_done, n + 1)
                act.copy(sel_bc[:, n % E, n // E, :], bank[4 + n % 2][:]).then_inc(bc_ready, 1)

            def gelu(i, jj):
                j = i * PER + jj
                slot = jj // (2 * HC)
                if jj % (2 * HC) == 0:
                    act.wait_ge(b1_ready, 2 * i + slot + 1)
                act.wait_ge(up_done, j + 1)
                bias = b1_now[:, slot, jj % HC:jj % HC + 1]
                act.activation(hid[:, jj % RING, :], bank[jj % RING][:], ACT.Gelu_apprx_tanh,
                               bias=bias).then_inc(gelu_done, 1)

            def body(i):
                for jj in range(PER):
                    gelu(i, jj)

            iterations(act, body)

        @block.vector
        def _(dve):
            steps = [0]

            def link(ins):
                steps[0] += 1
                ins.then_inc(dve_step, 1)
                dve.wait_ge(dve_step, steps[0])

            def norm_stats(src, mv, lo, hi):
                for t in range(lo, hi):
                    ins = dve.bn_stats(stats[:, t, :], src[:, t, :])
                    if t == hi - 1:
                        link(ins)
                    else:
                        steps[0] += 1
                        ins.then_inc(dve_step, 1)
                for t in range(lo, hi):
                    ins = dve.bn_aggr(mv[:, t, :], stats[:, t, :])
                return ins

            def normalise(dst, src, mv, rs, t):
                return dve.tensor_scalar(dst[:, t, :], src[:, t, :], mv[:, t, 0:1], rs[:, t:t + 1],
                                         ALU.subtract, ALU.mult)

            for h in range(NH):
                dve.wait_ge(ld_x[h], 16)
                norm_stats(x_sb, mv1, h * TH, (h + 1) * TH).then_inc(var1, 1)
            dve.wait_ge(index_ready, 3)
            link(dve.tensor_scalar(head_of[:], part_i[:], 31, 3, ALU.bitwise_and, ALU.logical_shift_right))
            dve.tensor_tensor(own_head[:], head_of[:], col_j[:], ALU.is_equal).then_inc(own_ready, 1)
            dve.wait_ge(ld_wkv, 16)
            dve.tensor_copy(wk_rep[:], wkv_sb[:, 0:D].rearrange("p (g c) -> p g c", g=G).unsqueeze(2)
                            .to_broadcast([P, G, 3, 32])).then_inc(rep_ready, 1)
            dve.wait_ge(ld_wq, 16)
            dve.tensor_copy(wq_rep[:], wq_sb[:].rearrange("p (g c) -> p g c", g=G).unsqueeze(2)
                            .to_broadcast([P, G, 3, 32])).then_inc(rep_ready, 1)
            for h in range(NH):
                dve.wait_ge(rstd1_ready, h + 1)
                for t in range(h * TH, (h + 1) * TH):
                    normalise(xn, x_sb, mv1, rstd1, t).then_inc(xn_ready, 1)

            dve.wait_ge(bias_ready, 1)
            dve.wait_ge(own_ready, 1)
            for g in range(G):
                dve.wait_ge(k_hi, g + 1)
                dve.scalar_tensor_tensor(out=k_mix[32:64, g, :], in0=bank[g][32:64, 0:KEYS],
                                         scalar=bias_cols[32:64, RK + g:RK + g + 1],
                                         in1=k_mix[32:64, g, :].bitcast(F32), op0=ALU.add,
                                         op1=ALU.subtract).then_inc(k_lo, 1)
                dve.wait_ge(k_lo, g + 1)
                for j in range(GH):
                    dve.tensor_scalar(k_blk[0:EXT, g, :, j, :], k_mix[:, g, :].rearrange("p (b k) -> p b k", b=B).bitcast(F32),
                                      own_head[0:EXT, j:j + 1], None, ALU.mult).then_inc(k_ready, 1)

            def b1_of(e, slot):
                cols = bias_cols[:, e * HC:(e + 1) * HC] if known(e) else bias_cols[:, bass.ds(e * HC, HC)]
                dve.tensor_copy(b1_now[:, slot, :], cols).then_inc(b1_ready, 1)

            def q_lo_of(h):
                for g in range(G):
                    n = G * h + g
                    dve.wait_ge(q_hi, n + 1)
                    rows = q_st[64:EXT, g, h * HT:(h + 1) * HT]
                    dve.scalar_tensor_tensor(out=rows, in0=bank[n % 4][64:EXT, :],
                                             scalar=bias_cols[64:EXT, RQ + g:RQ + g + 1],
                                             in1=rows.bitcast(F32), op0=ALU.add,
                                             op1=ALU.subtract).then_inc(q_lo, 1)

            def maxima(b):
                for t in range(TB * b, TB * (b + 1)):
                    for half in range(2):
                        n = 2 * t + half
                        dve.wait_ge(s_done, n + 1)
                        dve.tensor_reduce(nmax[:, t, 8 * half:8 * half + 8],
                                          bank[half][:].rearrange("p (a k) -> p a k", k=SK), AX.X, ALU.max,
                                          negate=True).then_inc(max_read, 1)
                dve.wait_ge(max_read, 2 * TB * (b + 1))
                t = slice(TB * b, TB * (b + 1))
                rows = nmax[:, t, :].rearrange("p t (g j) -> p t g j", g=G)
                link(dve.tensor_copy(nm_cols[:, t, :, 1:1 + GH], rows))
                dve.tensor_tensor(nm_cols[:, t, :, 1 + GH:1 + 2 * GH], rows, nm_cols[:, t, :, 1:1 + GH].bitcast(F32),
                                  ALU.subtract).then_inc(nm_ready, 1)

            def nm_rows(b):
                dve.wait_ge(nmT_done, b + 1)
                for g in range(2):
                    dve.tensor_copy(q_st[EXT:P, g, b * S:(b + 1) * S],
                                    bank[5][32 * g:32 * g + 32, 0:S]).then_inc(nmT_ready, 1)

            def normed_values(b):
                dve.wait_ge(pv_done, b + 1)
                pv = bank[4][:, 0:TB * PR * VW].rearrange("p (t r w) -> p t r w", t=TB, r=PR)
                link(dve.reciprocal(rsum[:, b % 2, :, :].rearrange("p t (r j) -> p t r j", r=PR),
                                    pv[:, :, :, 2 * HD:VW]))
                if b >= 2:
                    dve.wait_ge(attnT_done, b - 1)
                for t in range(TB):
                    ins = dve.tensor_tensor(
                        attn[:, b % 2, t, :].rearrange("p (r j e) -> p r j e", r=PR, j=2),
                        pv[:, t, :, 0:2 * HD].rearrange("p r (j e) -> p r j e", j=2),
                        rsum[:, b % 2, t, :].rearrange("p (r j) -> p r j", r=PR).unsqueeze(3)
                        .to_broadcast([P, PR, 2, HD]), ALU.mult)
                    ins.then_inc(attn_ready, 1)

            def residual(b):
                dve.wait_ge(proj_done, b + 1)
                dve.wait_ge(xb_ready, b // BH + 1)
                t = slice(TB * b, TB * (b + 1))
                dve.tensor_tensor(x1[:, t, :], bank[7][:, 0:TB * D].rearrange("p (t d) -> p t d", t=TB),
                                  xb[:, t, :], ALU.add).then_inc(x1_ready, 1)
                dve.wait_ge(x1_ready, b + 1)
                norm_stats(x1, mv2, TB * b, TB * (b + 1)).then_inc(var2, 1)

            def second_norm(b):
                dve.wait_ge(rstd2_ready, b + 1)
                for t in range(TB * b, TB * (b + 1)):
                    normalise(x2n, x1, mv2, rstd2, t).then_inc(x2n_ready, 1)

            def x2_lo(b):
                dve.wait_ge(x2hi_ready, b + 1)
                dve.wait_ge(x2T_ready, b + 1)
                c = slice(b * S, (b + 1) * S)
                dve.tensor_tensor(x2T_lo[:, c], x2T[:, c], x2T_hi[:, c].bitcast(F32), ALU.subtract).then_inc(x2lo_ready, 1)

            def logits(h):
                t = slice(h * TH, (h + 1) * TH)
                dve.wait_ge(gate_done, BH * (h + 1))
                dve.wait_ge(ld_bg, 16)
                link(dve.tensor_tensor(logit[:, t, :], bank[5 - h][:, S:S + TH * E].rearrange("p (t e) -> p t e", t=TH),
                                       bg_bc[:].unsqueeze(1).to_broadcast([P, TH, E]), ALU.add))
                link(dve.tensor_reduce(lmax[:, t], logit[:, t, :], AX.X, ALU.max))
                dve.tensor_tensor(logit[:, t, :], logit[:, t, :], lmax[:, t].unsqueeze(2).to_broadcast([P, TH, E]),
                                  ALU.subtract).then_inc(logit_ready, 1)

            def select(h):
                t = slice(h * TH, (h + 1) * TH)
                bc = lambda a: a.to_broadcast([P, TH, E])
                dve.wait_ge(prob_exp, h + 1)
                link(dve.tensor_reduce(psumv[:, t], prob[:, t, :], AX.X, ALU.add))
                link(dve.reciprocal(psumv[:, t], psumv[:, t]))
                link(dve.tensor_tensor(prob[:, t, :], prob[:, t, :], bc(psumv[:, t].unsqueeze(2)), ALU.mult))
                for u in range(h * TH, (h + 1) * TH):
                    link(dve.max(top[:, u, :], prob[:, u, :]))
                for u in range(h * TH, (h + 1) * TH):
                    link(dve.max_index(top_at[:, u, :], top[:, u, :], prob[:, u, :]))
                link(dve.tensor_tensor(first[:, t, :], col_e[:].unsqueeze(1).to_broadcast([P, TH, E]),
                                       bc(top_at[:, t, 0:1]), ALU.is_equal))
                link(dve.tensor_tensor(second[:, t, :], col_e[:].unsqueeze(1).to_broadcast([P, TH, E]),
                                       bc(top_at[:, t, 1:2]), ALU.is_equal))
                link(dve.tensor_tensor(first[:, t, :], first[:, t, :], second[:, t, :], ALU.add))
                link(dve.tensor_tensor(norm[:, t], top[:, t, 0], top[:, t, 1], ALU.add))
                link(dve.tensor_scalar(norm[:, t], norm[:, t], 1e-8, None, ALU.add))
                link(dve.reciprocal(norm[:, t], norm[:, t]))
                link(dve.tensor_tensor(sel[:, t, :], prob[:, t, :], first[:, t, :], ALU.mult))
                link(dve.tensor_tensor(sel[:, t, :], sel[:, t, :], bc(norm[:, t].unsqueeze(2)), ALU.mult))
                link(dve.tensor_copy(sel_parts[:, t, 0:E], sel[:, t, :]))
                dve.tensor_tensor(sel_parts[:, t, E:2 * E], sel[:, t, :], sel_parts[:, t, 0:E].bitcast(F32),
                                  ALU.subtract).then_inc(sel_ready, 1)

            for e in range(2):
                b1_of(e, e)
            q_lo_of(0)
            dve.wait_ge(v_done, 1)
            dve.wait_ge(ld_bv, 16)
            dve.wait_ge(fill_ready, 4)
            for j in range(2):
                rows = slice(SK * j, SK * (j + 1))
                cols = slice(HD * j, HD * (j + 1))
                for b in range(B):
                    dve.tensor_tensor(v_blk[rows, b, :, cols],
                                      bank[5][rows, b * D:(b + 1) * D].rearrange("p (r w) -> p r w", r=PR)[:, :, cols],
                                      bv_bc[rows, :].rearrange("p (r w) -> p r w", r=PR)[:, :, cols],
                                      ALU.add).then_inc(v_ready, 1)
            q_lo_of(1)
            for b in range(B + 3):
                if b < B:
                    maxima(b)
                    nm_rows(b)
                if 0 <= b - 1 < B:
                    normed_values(b - 1)
                    residual(b - 1)
                    second_norm(b - 1)
                if 0 <= b - 2 < B:
                    x2_lo(b - 2)
                if b - 3 in (BH - 1, B - 1):
                    logits((b - 3) // BH)
            for h in range(NH):
                select(h)
            dve.wait_ge(pick_ready, 1)
            dve.tensor_copy(pick_r[:], pick[:]).then_inc(pick_r_ready, 1)
            dve.wait_ge(bc_ready, NH * E)

            def scale(i, uu):
                unit = 2 * NH * i + uu
                e = 2 * i + uu // NH
                c = uu % NH
                dve.wait_ge(down_done, HC * (unit + 1))
                after(dve, y_added, unit - 1)
                bias = bias_cols[:, R2 + e:R2 + e + 1] if known(i) else bias_cols[:, bass.ds(R2 + e, 1)]
                w = sel_bc[:, e, c, :] if known(i) else sel_bc[:, bass.ds(e, 1), c, :].rearrange("p a n -> p (a n)")
                dve.scalar_tensor_tensor(out=part[:, c, :], in0=bank[4 + c][:], scalar=bias, in1=w,
                                         op0=ALU.add, op1=ALU.mult).then_inc(y_scaled, 1)

            def body(i):
                for jj in range(PER):
                    j = i * PER + jj
                    dve.wait_ge(gelu_done, j + 1)
                    dve.tensor_copy(hid_hi[:, jj % RING, :], hid[:, jj % RING, :]).then_inc(hid_split, 1)
                    if jj % HC < HC - 1:
                        dve.wait_ge(hid_split, j + 1)
                        hid_low(dve, jj).then_inc(lo_dve, 1)
                    e = 2 * i + jj // (2 * HC) + 1
                    if jj % (2 * HC) in (4, 6) and not (known(i) and not 2 <= e < E):
                        which = jj % (2 * HC) // 2 - 2
                        dve.wait_ge(down_done, 2 * HC * (e - 1))
                        dve.tensor_copy(w_hi[:, 1 - jj // (2 * HC), which, :], weight(e, which)).then_inc(wsplit_hi, 1)
                        if which == 0:
                            dve.wait_ge(gelu_done, 2 * HC * (e - 1))
                            b1_of(e, 1 - jj // (2 * HC))
                    if jj % HC == 0:
                        uu = jj // HC - 2
                        if uu >= 0:
                            scale(i, uu)
                        elif not known(i) or i > 0:
                            scale(i - 1, 2 * NH + uu)

            iterations(dve, body)
            for c in range(NH):
                scale(ITER - 1, NH + c)
            for h in range(NH):
                dve.wait_ge(outT_done, h + 1)
                t = slice(h * TH, (h + 1) * TH)
                dve.tensor_tensor(y_out[:, t, :], bank[6 + h][:].rearrange("p (t d) -> p t d", t=TH), x1[:, t, :],
                                  ALU.add).then_inc(out_ready, 1)

        @block.tensor
        def _(pe):
            pe.wait_ge(ident_ready, 1)
            pe.wait_ge(ld_ctx, 16)
            for c in range(KEYS // P):
                ins = pe.transpose(bank[6][:, c * P:(c + 1) * P], ctx_sb[:, c, :], ident[:])
            ins.then_inc(ctxT_done, 1)
            pe.wait_ge(ld_bias, 16 * 8)
            pe.transpose(bank[7][:, 0:NR], bias_rows[:], ident[0:NR, 0:NR]).then_inc(biasT_done, 1)
            pe.wait_ge(ctxT_ready, 2)
            pe.wait_ge(rep_ready, 1)
            for g in range(G):
                pe.matmul(bank[g][0:EXT, 0:KEYS], wk_rep[:, g, :, :].rearrange("p a c -> p (a c)"), ctxT[:, :, 0, :],
                          start=True, stop=True).then_inc(k_done, 1)
            for b in range(B):
                ins = pe.matmul(bank[5][:, b * D:(b + 1) * D], ctxT[:, b, :, :].rearrange("p a k -> p (a k)"),
                                wkv_sb[:, D:2 * D], start=True, stop=True)
            ins.then_inc(v_done, 1)

            def queries(h):
                pe.wait_ge(xn_ready, TH * (h + 1))
                if h == 0:
                    pe.wait_ge(bias_ready, 1)
                for t in range(TH):
                    ins = pe.transpose(bank[7 - h][:, t * P:(t + 1) * P], xn[:, h * TH + t, :], ident[:])
                ins.then_inc(xnT_done, 1)
                pe.wait_ge(xnT_ready, h + 1)
                pe.wait_ge(rep_ready, 2)
                for g in range(G):
                    n = G * h + g
                    if h == 0:
                        pe.wait_ge(k_lo, g + 1)
                    else:
                        pe.wait_ge(q_lo, n - G + 1)
                    pe.matmul(bank[n % 4][0:EXT, :], wq_rep[:, g, :, :].rearrange("p a c -> p (a c)"), xnT[:, h, :],
                              start=True, stop=True).then_inc(q_done, 1)

            def scores(b):
                for t in range(TB * b, TB * (b + 1)):
                    for half in range(2):
                        n = 2 * t + half
                        if n >= 2:
                            pe.wait_ge(max_read, n - 1)
                        for gg in range(2):
                            g = 2 * half + gg
                            ins = pe.matmul(bank[half][:, gg * 256:(gg + 1) * 256], q_st[:, g, t * P:(t + 1) * P],
                                            k_blk[:, g, b, :, :].rearrange("p j k -> p (j k)"), start=True, stop=True)
                        ins.then_inc(s_done, 1)

            def max_rows(b):
                pe.wait_ge(nm_ready, b + 1)
                if b:
                    pe.wait_ge(nmT_ready, G * b)
                else:
                    pe.wait_ge(v_ready, 2 * B)
                for t in range(TB):
                    ins = pe.transpose(bank[5][:, t * P:(t + 1) * P],
                                       nm_cols[:, TB * b + t, :, :].rearrange("p g r -> p (g r)").bitcast(F32), ident[:])
                ins.then_inc(nmT_done, 1)

            def scoresT(b):
                pe.wait_ge(nmT_ready, G * (b + 1))
                for n in range(PR // 2):
                    m = PR // 2 * b + n
                    if m >= 2:
                        pe.wait_ge(exp_done, m - 1)
                    for k in range(2):
                        pair = 2 * n + k
                        g, j = pair // 2, 2 * (pair % 2)
                        ins = pe.matmul(bank[2 + n % 2][:, k * S:(k + 1) * S], k_blk[:, g, b, j:j + 2, :].rearrange("p j k -> p (j k)"),
                                        q_st[:, g, b * S:(b + 1) * S], start=True, stop=True)
                    ins.then_inc(st_done, 1)

            def values(b):
                if b:
                    pe.wait_ge(attnT_ready, b)
                for t in range(TB):
                    for pair in range(PR):
                        pe.wait_ge(exp_done, PR // 2 * b + pair // 2 + 1)
                        at = (t * PR + pair) * VW
                        ins = pe.matmul(bank[4][:, at:at + VW], probsT[:, b % 2, pair, t * P:(t + 1) * P],
                                        v_blk[:, b, pair, :], start=True, stop=True)
                ins.then_inc(pv_done, 1)

            def attn_turn(b):
                pe.wait_ge(attn_ready, TB * (b + 1))
                for t in range(TB):
                    ins = pe.transpose(bank[4][:, t * P:(t + 1) * P], attn[:, b % 2, t, :], ident[:])
                ins.then_inc(attnT_done, 1)

            def project(b):
                pe.wait_ge(attnT_ready, b + 1)
                pe.wait_ge(ld_wo, 16)
                if b == 0:
                    pe.wait_ge(xnT_ready, 1)
                else:
                    pe.wait_ge(x1_ready, b)
                for t in range(TB):
                    ins = pe.matmul(bank[7][:, t * D:(t + 1) * D], attnT[:, b % 2, t * P:(t + 1) * P], wo_sb[:],
                                    start=True, stop=True)
                ins.then_inc(proj_done, 1)

            def turn_x2(b):
                pe.wait_ge(x2n_ready, TB * (b + 1))
                if b:
                    pe.wait_ge(x2T_ready, b)
                else:
                    pe.wait_ge(xnT_ready, 2)
                for t in range(TB):
                    ins = pe.transpose(bank[6][:, t * P:(t + 1) * P], x2n[:, TB * b + t, :], ident[:])
                ins.then_inc(x2T_done, 1)

            def gates(b):
                pe.wait_ge(x2T_ready, b + 1)
                pe.wait_ge(ld_wg, 16)
                h = b // BH
                for t in range(TB * b, TB * (b + 1)):
                    at = S + (t - h * TH) * E
                    ins = pe.matmul(bank[5 - h][:, at:at + E], x2T[:, t * P:(t + 1) * P], wg_sb[:], start=True, stop=True)
                ins.then_inc(gate_done, 1)

            queries(0)
            pe.wait_ge(q_lo, G)
            queries(1)
            pe.wait_ge(q_lo, 2 * G)
            pe.wait_ge(k_ready, G * GH)
            pe.wait_ge(ext_ready, G)
            pe.wait_ge(fill_ready, 4)
            for b in range(B + 3):
                if b < B:
                    scores(b)
                    max_rows(b)
                if 0 <= b - 1 < B:
                    attn_turn(b - 1)
                    project(b - 1)
                if b < B:
                    scoresT(b)
                    values(b)
                if 0 <= b - 2 < B:
                    turn_x2(b - 2)
                if 0 <= b - 2 < B:
                    gates(b - 2)

            def up(i, jj):
                j = i * PER + jj
                slot = jj // (2 * HC)
                c = jj // HC % NH
                hc = jj % HC
                if jj % (2 * HC) == 0:
                    pe.wait_ge(wsplit, 2 * (2 * i + slot) + 1)
                if known(i) and i == 0 and jj in (0, HC):
                    pe.wait_ge(x2hi_ready, BH * (c + 1))
                    pe.wait_ge(x2lo_ready, BH * (c + 1))
                after(pe, gelu_done, j - RING + 1)
                w = slice(hc * P, (hc + 1) * P)
                q = slice(c * HT, (c + 1) * HT)
                for n, (a, m) in enumerate(((w_hi, x2T_hi), (w_hi, x2T_lo), (w_lo, x2T_hi))):
                    ins = pe.matmul(bank[jj % RING][:], a[:, slot, 0, w], m[:, q], start=(n == 0), stop=(n == 2))
                ins.then_inc(up_done, 1)

            def down(i, jj):
                j = i * PER + jj
                slot = jj // (2 * HC)
                c = jj // HC % NH
                hc = jj % HC
                if jj % (2 * HC) == 0:
                    pe.wait_ge(wsplit, 2 * (2 * i + slot) + 2)
                if hc == 0:
                    after(pe, y_scaled, 2 * NH * i + jj // HC - 1)
                wait_lo(pe, i * 2 * NH + jj // HC, hc)
                w = slice(hc * D, (hc + 1) * D)
                for n, (a, m) in enumerate(((w_hi, hid_hi), (w_hi, hid_lo), (w_lo, hid_hi))):
                    ins = pe.matmul(bank[4 + c][:], a[:, slot, 1, w], m[:, jj % RING, :],
                                    start=(hc == 0 and n == 0), stop=(hc == HC - 1 and n == 2))
                ins.then_inc(down_done, 1)

            for jj in range(AHEAD):
                up(0, jj)
            for h in range(NH):
                pe.wait_ge(sel_ready, h + 1)
                if h == 0:
                    pe.wait_ge(x1_ready, B)
                for t in range(TH):
                    ins = pe.transpose(bank[7 - h][0:2 * E, t * P:(t + 1) * P],
                                       sel_parts[:, h * TH + t, :].bitcast(F32), ident[:])
                ins.then_inc(selT_done, 1)
            pe.wait_ge(pick_r_ready, 1)
            for n in range(NH * E):
                pe.wait_ge(selT_ready, n // E + 1)
                if n >= 2:
                    pe.wait_ge(bc_ready, n - 1)
                pe.matmul(bank[4 + n % 2][:], pick_r[:, n % E, :], selT[:, n // E, :], start=True, stop=True).then_inc(bc_done, 1)
            pe.wait_ge(bc_ready, NH * E)

            def body(i):
                for jj in range(PER):
                    down(i, jj)
                    if jj + AHEAD < PER:
                        up(i, jj + AHEAD)
                    elif not known(i) or i < ITER - 1:
                        up(i + 1, jj + AHEAD - PER)

            iterations(pe, body)
            for h in range(NH):
                pe.wait_ge(y_added, NH * (E - 1) + h + 1)
                for t in range(TH):
                    ins = pe.transpose(bank[6 + h][:, t * P:(t + 1) * P], acc[:, h, t * P:(t + 1) * P], ident[:])
                ins.then_inc(outT_done, 1)

    return nc


INS = ["x", "ctx_1024", "mask_BxS2_bk0", "L0_xattn_Wq", "L0_xattn_bq", "L0_xattn_Wkv", "L0_xattn_bkv",
       "L0_xattn_Wo", "L0_xattn_bo", "L0_ffn_Wg", "L0_ffn_bg", "L0_ffn_W1", "L0_ffn_b1", "L0_ffn_W2", "L0_ffn_b2"]


def kernel(**inputs):
    import numpy as np
    import concourse.bacc as bacc
    from concourse.bass_utils import run_bass_kernel_spmd

    nc = bacc.Bacc("TRN2", target_bir_lowering=False, num_devices=1)
    arrays, args = {}, []
    for name in INS:
        a = np.ascontiguousarray(inputs[name])
        arrays[f"in_{name}"] = a
        args.append(nc.dram_tensor(f"in_{name}", a.shape, mybir.dt.from_np(a.dtype), kind="ExternalInput").ap())
    args.append(nc.dram_tensor("out_y", arrays["in_x"].shape, F32, kind="ExternalOutput").ap())
    build(nc, *args)
    r = run_bass_kernel_spmd(nc, [arrays], core_ids=[0])
    return r.results[0]["out_y"]
```

```python
from contextlib import ExitStack

import concourse.bass as bass
from concourse import mybir

F32 = mybir.dt.float32
F32R = mybir.dt.float32r
U8 = mybir.dt.uint8
I32 = mybir.dt.int32
U32 = mybir.dt.uint32
ALU = mybir.AluOpType
ACT = mybir.ActivationFunctionType
AX = mybir.AxisListType

P = 128
EPS = 1e-5
MASKED = -1e30
HEADS = 16


def build(nc, x, ctx_in, mask, Wq, bq, Wkv, bkv, Wo, bo, Wg, bg, W1, b1, W2, b2, out):
    B, S, D = x.shape
    SK = ctx_in.shape[1]
    E, _, HID = W1.shape
    T = B * S // P
    TB = S // P
    NH = 2
    TH = T // NH
    HT = TH * P
    BH = B // NH
    HC = HID // P
    HD = D // HEADS
    SCALE = float(HD) ** -0.5
    G = 4
    GH = HEADS // G
    PR = HEADS // 2
    KEYS = B * SK
    EXT = 96
    HALF = P // 2
    VS = P + 2 * HD
    assert D == P and GH * HD == 32 and 2 * SK == P and TB == 2 and HT == 512 and KEYS == 256

    with ExitStack() as stack:
        def sb(name, shape, dt=F32):
            return stack.enter_context(nc.sbuf_tensor(name, shape, dt))

        def sem(name):
            return stack.enter_context(nc.semaphore(name))

        bank = [stack.enter_context(nc.psum_tensor(f"bank{i}", [P, 512], F32)) for i in range(8)]

        x_sb = sb("x_sb", [P, T, D])
        ctx_sb = sb("ctx_sb", [P, KEYS // P, D])
        wq_sb = sb("wq_sb", [P, D])
        wkv_sb = sb("wkv_sb", [P, 2 * D])
        wo_sb = sb("wo_sb", [P, D])
        wg_sb = sb("wg_sb", [P, E])
        w1_sb = sb("w1_sb", [P, E, HID])
        w2_sb = sb("w2_sb", [P, E, HC * D])
        NB1 = E * HC
        R2, RQ, RK, NR = NB1, NB1 + E, NB1 + E + G, NB1 + E + 2 * G
        bias_rows = sb("bias_rows", [NR, P])
        warm = sb("warm", [P, 1])
        bias_cols = sb("bias_cols", [P, NR])
        bv_bc = sb("bv_bc", [P, D])
        bo_bc = sb("bo_bc", [P, D])
        bg_bc = sb("bg_bc", [P, E])
        mask_row = sb("mask_row", [P, KEYS], U8)

        mask_add = sb("mask_add", [P, KEYS])

        ident = sb("ident", [P, P])
        part_i = sb("part_i", [P, GH], I32)
        head_of = sb("head_of", [P, GH], I32)
        col_j = sb("col_j", [P, GH], I32)
        own_head = sb("own_head", [P, GH])
        minus_half = sb("minus_half", [P, T])
        col_e = sb("col_e", [P, E], I32)
        pick = sb("pick", [2 * E, E])

        wq_rep = sb("wq_rep", [P, G, EXT + 1])
        wk_rep = sb("wk_rep", [P, G, 3, 32])
        ctxT = sb("ctxT", [P, B, 2, SK])
        k_mix = sb("k_mix", [EXT, G, KEYS], F32R)
        k_blk = sb("k_blk", [P, G, B, GH, SK], F32R)
        v_blk = sb("v_blk", [P, B, PR * VS])
        stats = sb("stats", [P, T, 6])
        mv1 = sb("mv1", [P, T, 2])
        rstd1 = sb("rstd1", [P, T])
        xn = sb("xn", [P, T, D])
        xnT = sb("xnT", [P, NH, HT])
        q_st = sb("q_st", [P, G, T * P], F32R)
        nmax = sb("nmax", [P, T, HEADS])
        nm_cols = sb("nm_cols", [P, T, G, 32], F32R)
        probs_mem = sb("probs_mem", [P, 2 * PR * S])
        probsT = probs_mem[:].rearrange("p (r a q) -> p r a q", r=2, a=PR)
        ext_sel = probs_mem[:, 0:GH * KEYS].rearrange("p (b j k) -> p b j k", b=B, j=GH)
        sumT = sb("sumT", [P, S])
        attnT = sb("attnT", [P, 2, S])
        xb = sb("xb", [P, T, D])
        x1 = sb("x1", [P, T, D])

        mv2 = sb("mv2", [P, T, 2])
        rstd2 = sb("rstd2", [P, T])
        x2n = xn
        x2T = xnT[:].rearrange("p h q -> p (h q)")
        x2T_hi = sb("x2T_hi", [P, T * P], F32R)
        x2T_lo = sb("x2T_lo", [P, T * P], F32R)
        logit = sb("logit", [P, T, E])
        lmax = sb("lmax", [P, T])
        prob = sb("prob", [P, T, E])
        psumv = sb("psumv", [P, T])
        top = sb("top", [P, T, E])
        top_at = sb("top_at", [P, T, E], U32)
        first = sb("first", [P, T, E])
        second = sb("second", [P, T, E])
        norm = sb("norm", [P, T])
        sel = sb("sel", [P, T, E])
        sel_parts = sb("sel_parts", [P, T, 2 * E], F32R)
        selT = sb("selT", [2 * E, NH, HT], F32R)

        w_hi = sb("w_hi", [P, 2, 2, HID], F32R)
        w_lo = sb("w_lo", [P, 2, 2, HID], F32R)
        RING = 4
        hid = probs_mem[:, 0:RING * HT].rearrange("p (r q) -> p r q", r=RING)
        part = probs_mem[:, RING * HT:(RING + 2) * HT].rearrange("p (r q) -> p r q", r=2)
        k_mem = k_blk[:].rearrange("p g b j k -> p (g b j k)")
        hid_hi = k_mem[:, 0:RING * HT].rearrange("p (r q) -> p r q", r=RING)
        hid_lo = k_mem[:, RING * HT:2 * RING * HT].rearrange("p (r q) -> p r q", r=RING)
        sel_now = sb("sel_now", [P, NH, HT])
        acc = sb("acc", [P, NH, HT])
        b1_now = sb("b1_now", [P, 2, HC])
        pick_now = sb("pick_now", [2 * E, 2, P], F32R)
        y_out = x_sb

        ld_x = [sem(f"ld_x{h}") for h in range(NH)]
        ld_ctx, ld_wq, ld_wkv, ld_wo, ld_wg = (sem(n) for n in ("ld_ctx", "ld_wq", "ld_wkv", "ld_wo", "ld_wg"))
        ld_w = [sem(f"ld_w{e}") for e in range(E)]
        ld_bias, ld_bv, ld_bo, ld_bg, ld_mask = (sem(n) for n in ("ld_bias", "ld_bv", "ld_bo", "ld_bg", "ld_mask"))
        stored = sem("stored")
        pool_step = sem("pool_step")
        half_ready = sem("half_ready")
        zeroed = sem("zeroed")
        ident_ready = sem("ident_ready")
        pick_ready = sem("pick_ready")
        index_ready = sem("index_ready")
        fill_ready = sem("fill_ready")
        ext_ready = sem("ext_ready")
        ext_copied = sem("ext_copied")
        xb_ready = sem("xb_ready")
        dve_step = sem("dve_step")
        rep_ready = sem("rep_ready")
        ones_ready = sem("ones_ready")
        own_ready = sem("own_ready")
        biasT_done, bias_ready = sem("biasT_done"), sem("bias_ready")
        ctxT_done, ctxT_ready = sem("ctxT_done"), sem("ctxT_ready")
        k_done, k_hi, k_lo = (sem(n) for n in ("k_done", "k_hi", "k_lo"))
        k_blk_dve, k_blk_act = sem("k_blk_dve"), sem("k_blk_act")
        v_filled, v_done, v_ready = sem("v_filled"), sem("v_done"), sem("v_ready")
        var1, rstd1_ready, xn_ready = sem("var1"), sem("rstd1_ready"), sem("xn_ready")
        xnT_done, xnT_ready = sem("xnT_done"), sem("xnT_ready")
        q_done, q_hi, q_lo = sem("q_done"), sem("q_hi"), sem("q_lo")
        s_done, max_read, nm_ready = sem("s_done"), sem("max_read"), sem("nm_ready")
        nmT_done, nmT_ready = sem("nmT_done"), sem("nmT_ready")
        st_done, exp_done = sem("st_done"), sem("exp_done")
        pv_done, sums_ready, attn_ready = sem("pv_done"), sem("sums_ready"), sem("attn_ready")
        proj_done, x1_ready = sem("proj_done"), sem("x1_ready")
        var2, rstd2_ready, x2n_ready = sem("var2"), sem("rstd2_ready"), sem("x2n_ready")
        x2T_done, x2T_ready, x2hi_ready, x2lo_ready = (sem(n) for n in ("x2T_done", "x2T_ready", "x2hi_ready", "x2lo_ready"))
        gate_done, logit_ready, prob_exp, sel_ready = (sem(n) for n in ("gate_done", "logit_ready", "prob_exp", "sel_ready"))
        selT_done, selT_ready = sem("selT_done"), sem("selT_ready")
        acc_zero = sem("acc_zero")
        wsplit_hi = sem("wsplit_hi")
        wsplit = sem("wsplit")
        up_done, gelu_done = sem("up_done"), sem("gelu_done")
        staged = sem("staged")
        hid_split, lo_dve, lo_pool, down_done = (sem(n) for n in ("hid_split", "lo_dve", "lo_pool", "down_done"))
        bc_done, sel_copied = sem("bc_done"), sem("sel_copied")
        y_scaled, y_added = sem("y_scaled"), sem("y_added")
        outT_done, out_ready = sem("outT_done"), sem("out_ready")

        x_t = x.rearrange("b (t p) d -> p (b t) d", p=P)
        out_t = out.rearrange("b (t p) d -> p (b t) d", p=P)

        block = stack.enter_context(nc.Block())

        PER = 2 * NH * HC
        ITER = E // 2
        AHEAD = RING
        known = lambda v: isinstance(v, int)

        def k_bank(g, lo, hi):
            return bank[(2, 3, 4, 6)[g]][lo:hi, 0:KEYS]

        Q_BANKS = ((0, 1, 4, 6), (2, 3, 4, 6))
        v_diag = v_blk[:].rearrange("p b (r w) -> p b r w", r=PR)
        V_FILLS = 5
        WARM_UP = 8
        PV = (slice(0, HALF), slice(HALF, P))
        PS = (slice(HALF, P), slice(0, HALF))

        def after(eng, s, value):
            if not known(value) or value > 0:
                eng.wait_ge(s, value)

        def wait_lo(eng, unit, hc):
            if hc == HC - 1:
                after(eng, lo_pool, unit + 1)
            else:
                after(eng, lo_dve, (HC - 1) * unit + hc + 1) if not known(unit) or unit >= 0 else None

        def hid_low(eng, jj):
            return eng.tensor_tensor(hid_lo[:, jj % RING, :], hid[:, jj % RING, :],
                                     hid_hi[:, jj % RING, :].bitcast(F32), ALU.subtract)

        def weight(e, which):
            w = (w1_sb, w2_sb)[which]
            return w[:, e, :] if known(e) else w[:, bass.ds(e, 1), :].rearrange("p a n -> p (a n)")

        def iterations(eng, body):
            body(0)
            with eng.Fori(1, ITER - 1) as i:
                body(i)
            body(ITER - 1)

        @block.sync
        def _(sp):
            sp.dma_start(x_sb[:, 0:TH, :], x_t[:, 0:TH, :]).then_inc(ld_x[0], 16)
            sp.dma_start(wkv_sb[:], Wkv).then_inc(ld_wkv, 16)
            sp.dma_start(wq_sb[:], Wq).then_inc(ld_wq, 16)
            sp.dma_start(x_sb[:, TH:T, :], x_t[:, TH:T, :]).then_inc(ld_x[1], 16)
            sp.wait_ge(zeroed, 1)
            sp.dma_start(mask_row[EXT:EXT + 1, :],
                         mask.rearrange("(a b) k -> a (b k)", a=1)).then_inc(ld_mask, 16)
            sp.dma_start(bv_bc[:], bkv[D:2 * D].rearrange("(a d) -> a d", a=1).to_broadcast([P, D])).then_inc(ld_bv, 16)
            sp.dma_start(wo_sb[:], Wo).then_inc(ld_wo, 16)
            sp.dma_start(bo_bc[:], bo.rearrange("(a d) -> a d", a=1).to_broadcast([P, D])).then_inc(ld_bo, 16)
            sp.dma_start(wg_sb[:], Wg).then_inc(ld_wg, 16)
            sp.dma_start(bg_bc[:], bg.rearrange("(a d) -> a d", a=1).to_broadcast([P, E])).then_inc(ld_bg, 16)
            for e in range(E):
                sp.dma_start(w1_sb[:, e, :], W1[e]).then_inc(ld_w[e], 16)
                sp.dma_start(w2_sb[:, e, :].rearrange("p (c f) -> p c f", c=HC),
                             W2[e].rearrange("(c p) f -> p c f", p=P)).then_inc(ld_w[e], 16)
            for h in range(NH):
                sp.wait_ge(out_ready, h + 1)
                sp.dma_start(out_t[:, h * TH:(h + 1) * TH, :], y_out[:, h * TH:(h + 1) * TH, :]).then_inc(stored, 16)
            sp.wait_ge(stored, 16 * NH)

        @block.gpsimd
        def _(pool):
            steps = [0]

            def link(ins):
                steps[0] += 1
                ins.then_inc(pool_step, 1)
                pool.wait_ge(pool_step, steps[0])

            pool.memset(minus_half[:], -0.5).then_inc(half_ready, 1)
            pool.wait_ge(half_ready, 1)
            pool.memset(mask_row[EXT:P, :], 0).then_inc(zeroed, 1)
            pool.wait_ge(zeroed, 1)
            link(pool.memset(ident[:], 0.0))
            pool.affine_select(out=ident[:], in_=ident[:], compare_op=ALU.not_equal, fill=1.0, base=0,
                               pattern=[[-1, P]], channel_multiplier=1).then_inc(ident_ready, 1)
            pool.iota(part_i[:], pattern=[[0, GH]], base=0, channel_multiplier=1).then_inc(index_ready, 1)
            pool.iota(col_j[:], pattern=[[1, GH]], base=0, channel_multiplier=0).then_inc(index_ready, 1)
            pool.iota(col_e[:], pattern=[[1, E]], base=0, channel_multiplier=0).then_inc(index_ready, 1)
            pool.wait_ge(index_ready, 3)

            def rstd(mv, rs, lo, hi):
                link(pool.tensor_scalar(rs[:, lo:hi], mv[:, lo:hi, 1], EPS, 1.0, ALU.add, ALU.mult))
                return pool.tensor_tensor(rs[:, lo:hi], rs[:, lo:hi], minus_half[:, lo:hi], ALU.pow)

            ext = ext_sel[EXT:P, :, :, :]
            def own_ones(first_row):
                return pool.affine_select(out=ext, in_=ext, compare_op=ALU.not_equal, fill=1.0, base=-first_row,
                                          pattern=[[0, B], [-1, GH], [0, SK]], channel_multiplier=1)

            link(pool.memset(ext, 0.0))
            link(own_ones(1))
            pool.wait_ge(var1, 1)
            rstd(mv1, rstd1, 0, TH).then_inc(rstd1_ready, 1)
            pool.wait_ge(rstd1_ready, 1)
            link(own_ones(1 + GH))
            pool.wait_ge(ld_mask, 16)
            link(pool.tensor_scalar(mask_add[EXT:P, :], mask_row[EXT:P, :], MASKED, 1.0, ALU.mult, ALU.mult))
            pool.tensor_tensor(k_blk[EXT:P, 0, :, :, :], ext, mask_add[EXT:P, :].rearrange("p (b k) -> p b k", b=B)
                               .unsqueeze(2).to_broadcast([P - EXT, B, GH, SK]), ALU.add).then_inc(ext_ready, 1)
            pool.wait_ge(ext_ready, 1)
            pool.dma_start(k_blk[EXT:P, 1:G, :, :, :].rearrange("p g b j k -> p g (b j k)"),
                           k_blk[EXT:P, 0:1, :, :, :].rearrange("p g b j k -> p g (b j k)")
                           .to_broadcast([P - EXT, G - 1, KEYS * GH])).then_inc(ext_copied, 16)
            pool.wait_ge(var1, 2)
            rstd(mv1, rstd1, TH, T).then_inc(rstd1_ready, 1)
            link(pool.memset(nm_cols[:].bitcast(F32), 0.0))
            pool.memset(nm_cols[:, :, :, 0:1].bitcast(F32), 1.0).then_inc(fill_ready, 1)
            pool.wait_ge(fill_ready, 1)
            pool.memset(v_blk[:], 0.0).then_inc(v_filled, 1)
            fills = 1
            for j in range(2):
                rows = slice(SK * j, SK * (j + 1))
                for r, at in ((0, HALF + HD * j), (PR // 2 - 1, VS - HALF + HD * j)):
                    pool.wait_ge(v_filled, fills)
                    pool.memset(v_diag[rows, :, r:r + PR // 2, at:at + HD], 1.0).then_inc(v_filled, 1)
                    fills += 1
            assert fills == V_FILLS
            pool.wait_ge(v_filled, fills)
            pool.wait_ge(ld_bo, 16)
            for h in range(NH):
                pool.wait_ge(ld_x[h], 16)
                t = slice(h * TH, (h + 1) * TH)
                pool.tensor_tensor(xb[:, t, :], x_sb[:, t, :],
                                   bo_bc[:].unsqueeze(1).to_broadcast([P, TH, D]), ALU.add).then_inc(xb_ready, 1)

            def weight_lo(e, slot, which):
                pool.wait_ge(wsplit_hi, 2 * e + which + 1)
                pool.tensor_tensor(w_lo[:, slot, which, :], weight(e, which), w_hi[:, slot, which, :].bitcast(F32),
                                   ALU.subtract).then_inc(wsplit, 1)

            pool.memset(acc[:], 0.0).then_inc(acc_zero, 1)
            for b in range(B):
                if b < 2:
                    pool.wait_ge(ld_w[b], 32)
                    for which in range(2):
                        pool.tensor_scalar(w_hi[:, b, which, :], weight(b, which), 1.0, 1.0, ALU.mult, ALU.mult).then_inc(wsplit_hi, 1)
                        weight_lo(b, b, which)
                pool.wait_ge(var2, b + 1)
                rstd(mv2, rstd2, TB * b, TB * (b + 1)).then_inc(rstd2_ready, 1)
            for e in range(2, E):
                pool.wait_ge(ld_w[e], 32)
            pool.wait_ge(acc_zero, 1)

            def body(i):
                for jj in range(PER):
                    j = i * PER + jj
                    slot = jj // (2 * HC)
                    if jj % HC == HC - 1:
                        pool.wait_ge(hid_split, j + 1)
                        hid_low(pool, jj).then_inc(lo_pool, 1)
                    e = 2 * i + slot + 1
                    if jj % (2 * HC) in (4, 6) and not (known(i) and not 2 <= e < E):
                        weight_lo(e, 1 - slot, jj % (2 * HC) // 2 - 2)
                    if jj % HC == 1:
                        unit = 2 * NH * i + jj // HC - 2
                        if not known(unit) or unit >= 0:
                            add(unit, jj // HC % 2)

            def add(unit, c):
                pool.wait_ge(y_scaled, unit + 1)
                after(pool, y_added, unit - 1)
                pool.tensor_tensor(acc[:, c, :], acc[:, c, :], part[:, c, :], ALU.add).then_inc(y_added, 1)

            iterations(pool, body)
            for c in range(NH):
                add(NH * (E - 1) + c, c)

        @block.scalar
        def _(act):
            act.dma_start(ctx_sb[:], ctx_in.rearrange("b k d -> (b k) d").rearrange("(t p) d -> p t d", p=P)).then_inc(ld_ctx, 16)
            act.wait_ge(half_ready, 1)
            act.activation(warm[:], minus_half[:, 0:1], ACT.Exp)
            for r, b_in in ((RK, bkv[0:D]), (RQ, bq)):
                act.dma_start(bias_rows[r:r + G, :].rearrange("g (a c) -> g a c", a=4),
                              b_in.rearrange("(g c) -> g c", g=G).unsqueeze(1).to_broadcast([G, 4, 32])).then_inc(ld_bias, 16)
            act.dma_start(bias_rows[0:NB1, :], b1.rearrange("e (c p) -> (e c) p", p=P)).then_inc(ld_bias, 16)
            act.dma_start(bias_rows[R2:R2 + E, :], b2).then_inc(ld_bias, 16)

            act.wait_ge(ctxT_done, 1)
            for c in range(2):
                act.copy(ctxT[:, :, c, :], bank[6][:, 0:KEYS].rearrange("p (b k) -> p b k", b=B)).then_inc(ctxT_ready, 1)
            act.wait_ge(biasT_done, 1)
            act.copy(bias_cols[:], bank[7][:, 0:NR]).then_inc(bias_ready, 1)
            act.wait_ge(bias_ready, 1)
            for g in range(G):
                act.wait_ge(k_done, g + 1)
                act.activation(k_mix[:, g, :], k_bank(g, 0, EXT), ACT.Identity,
                               bias=bias_cols[0:EXT, RK + g:RK + g + 1]).then_inc(k_hi, 1)

            act.wait_ge(ones_ready, 1)

            def xnT_of(h):
                act.wait_ge(xnT_done, h + 1)
                act.copy(xnT[:, h, :], bank[7][:]).then_inc(xnT_ready, 1)

            def q_hi_of(h, g):
                act.wait_ge(q_done, G * h + g + 1)
                act.activation(q_st[0:EXT + 1, g, h * HT:(h + 1) * HT], bank[Q_BANKS[h][g]][0:EXT + 1, :], ACT.Identity,
                               bias=bias_cols[0:EXT + 1, RQ + g:RQ + g + 1]).then_inc(q_hi, 1)

            def nm_rows(b):
                act.wait_ge(nmT_done, b + 1)
                for g in range(G):
                    act.copy(q_st[EXT:P, g, b * S:(b + 1) * S], bank[7][32 * g:32 * g + 32, 0:S]).then_inc(nmT_ready, 1)

            def exps(b):
                for n in range(PR // 2):
                    act.wait_ge(st_done, PR // 2 * b + n + 1)
                    if b >= 2 and n == 0:
                        act.wait_ge(pv_done, b - 1)
                    act.activation(probsT[:, b % 2, 2 * n:2 * n + 2, :], bank[2 + n % 2][:].rearrange("p (a q) -> p a q", a=2),
                                   ACT.Exp, scale=SCALE).then_inc(exp_done, 1)

            def sums_of(b):
                act.wait_ge(pv_done, b + 1)
                if b:
                    act.wait_ge(attn_ready, 2 * b)
                for gg in range(2):
                    act.copy(sumT[PV[gg], :], bank[4 + b % 2][PS[gg], gg * S:(gg + 1) * S]).then_inc(sums_ready, 1)

            def x2T_of(b):
                act.wait_ge(x2T_done, b + 1)
                act.copy(x2T_hi[:, b * S:(b + 1) * S], bank[6][:, 0:S]).then_inc(x2hi_ready, 1)
                act.copy(x2T[:, b * S:(b + 1) * S], bank[6][:, 0:S]).then_inc(x2T_ready, 1)

            def k_blocks(g):
                act.wait_ge(own_ready, 1)
                act.wait_ge(k_lo, g - 1)
                for j in range(GH):
                    act.activation(k_blk[0:EXT, g, :, j, :], k_mix[:, g, :].rearrange("p (b k) -> p b k", b=B).bitcast(F32),
                                   ACT.Copy, scale=own_head[0:EXT, j:j + 1]).then_inc(k_blk_act, 1)

            xnT_of(0)
            k_blocks(2)
            q_hi_of(0, 0)
            q_hi_of(0, 1)
            k_blocks(3)
            q_hi_of(0, 2)
            q_hi_of(0, 3)
            xnT_of(1)
            q_hi_of(1, 0)
            q_hi_of(1, 1)
            nm_rows(0)
            q_hi_of(1, 2)
            q_hi_of(1, 3)
            def gate_exp(h):
                t = slice(h * TH, (h + 1) * TH)
                act.wait_ge(logit_ready, h + 1)
                act.activation(prob[:, t, :], logit[:, t, :], ACT.Exp).then_inc(prob_exp, 1)

            for b in range(B):
                exps(b)
                if b >= 2:
                    x2T_of(b - 2)
                if b + 1 < B:
                    nm_rows(b + 1)
                if b == B - 1:
                    gate_exp(0)
                sums_of(b)
            x2T_of(B - 2)
            x2T_of(B - 1)
            gate_exp(1)

            def selT_of(h):
                act.wait_ge(selT_done, h + 1)
                act.copy(selT[:, h, :], bank[6 - h][0:2 * E, :]).then_inc(selT_ready, 1)

            selT_of(0)

            def weights_of_tokens(i, uu):
                unit = 2 * NH * i + uu
                act.wait_ge(bc_done, unit + 1)
                after(act, y_scaled, unit - 1)
                act.copy(sel_now[:, uu % NH, :], bank[6 + uu % NH][:]).then_inc(sel_copied, 1)

            def gelu(i, jj):
                j = i * PER + jj
                slot = jj // (2 * HC)
                if jj % (2 * HC) == 0:
                    act.wait_ge(staged, 2 * (2 * i + slot + 1))
                act.wait_ge(up_done, j + 1)
                bias = b1_now[:, slot, jj % HC:jj % HC + 1]
                act.activation(hid[:, jj % RING, :], bank[jj % RING][:], ACT.Gelu_apprx_tanh,
                               bias=bias).then_inc(gelu_done, 1)

            def body(i):
                for jj in range(PER):
                    gelu(i, jj)
                    if jj % HC == 1:
                        uu = jj // HC - 1
                        if uu >= 0:
                            weights_of_tokens(i, uu)
                        elif not known(i) or i > 0:
                            weights_of_tokens(i - 1, 2 * NH + uu)
                    if known(i) and i == 0 and jj == HC - 1:
                        selT_of(1)

            iterations(act, body)
            weights_of_tokens(ITER - 1, 2 * NH - 1)

        @block.vector
        def _(dve):
            steps = [0]

            def link(ins):
                steps[0] += 1
                ins.then_inc(dve_step, 1)
                dve.wait_ge(dve_step, steps[0])

            def count(ins):
                steps[0] += 1
                ins.then_inc(dve_step, 1)

            def norm_stats(src, mv, lo, hi):
                for t in range(lo, hi):
                    ins = dve.bn_stats(stats[:, t, :], src[:, t, :])
                    count(ins)
                dve.wait_ge(dve_step, steps[0])
                for t in range(lo, hi):
                    ins = dve.bn_aggr(mv[:, t, :], stats[:, t, :])
                return ins

            def normalise(dst, src, mv, rs, t):
                return dve.tensor_scalar(dst[:, t, :], src[:, t, :], mv[:, t, 0:1], rs[:, t:t + 1],
                                         ALU.subtract, ALU.mult)

            def first_stats(h):
                dve.wait_ge(ld_x[h], 16)
                norm_stats(x_sb, mv1, h * TH, (h + 1) * TH).then_inc(var1, 1)

            def first_norm(h):
                dve.wait_ge(rstd1_ready, h + 1)
                for t in range(h * TH, (h + 1) * TH):
                    normalise(xn, x_sb, mv1, rstd1, t).then_inc(xn_ready, 1)

            first_stats(0)
            dve.wait_ge(index_ready, 3)
            link(dve.tensor_scalar(head_of[:], part_i[:], 31, 3, ALU.bitwise_and, ALU.logical_shift_right))
            dve.tensor_tensor(own_head[:], head_of[:], col_j[:], ALU.is_equal).then_inc(own_ready, 1)
            dve.wait_ge(ld_wkv, 16)
            dve.tensor_copy(wk_rep[:], wkv_sb[:, 0:D].rearrange("p (g c) -> p g c", g=G).unsqueeze(2)
                            .to_broadcast([P, G, 3, 32])).then_inc(rep_ready, 1)
            first_norm(0)
            dve.wait_ge(ld_wq, 16)
            dve.memset(wq_rep[:, :, EXT:EXT + 1], 0.0).then_inc(rep_ready, 1)
            dve.tensor_copy(wq_rep[:, :, 0:EXT].rearrange("p g (a c) -> p g a c", a=3), wq_sb[:].rearrange("p (g c) -> p g c", g=G).unsqueeze(2)
                            .to_broadcast([P, G, 3, 32])).then_inc(rep_ready, 1)

            first_stats(1)
            dve.wait_ge(bias_ready, 1)
            dve.memset(bias_cols[EXT:EXT + 1, RQ:RQ + G], 1.0).then_inc(ones_ready, 1)
            dve.wait_ge(own_ready, 1)
            for g in (2, 3, 0, 1):
                dve.wait_ge(k_hi, g + 1)
                dve.scalar_tensor_tensor(out=k_mix[32:64, g, :], in0=k_bank(g, 32, 64),
                                         scalar=bias_cols[32:64, RK + g:RK + g + 1],
                                         in1=k_mix[32:64, g, :].bitcast(F32), op0=ALU.add,
                                         op1=ALU.subtract).then_inc(k_lo, 1)
            for g in range(2):
                if g == 0:
                    dve.wait_ge(k_lo, G)
                for j in range(GH):
                    dve.tensor_scalar(k_blk[0:EXT, g, :, j, :], k_mix[:, g, :].rearrange("p (b k) -> p b k", b=B).bitcast(F32),
                                      own_head[0:EXT, j:j + 1], None, ALU.mult).then_inc(k_blk_dve, 1)

            def stage(e, slot):
                cols = bias_cols[:, e * HC:(e + 1) * HC] if known(e) else bias_cols[:, bass.ds(e * HC, HC)]
                dve.tensor_copy(b1_now[:, slot, :], cols).then_inc(staged, 1)
                col = pick[:, e:e + 1] if known(e) else pick[:, bass.ds(e, 1)]
                dve.tensor_copy(pick_now[:, slot, :], col.to_broadcast([2 * E, P])).then_inc(staged, 1)

            def q_lo_of(h):
                for g in range(G):
                    n = G * h + g
                    dve.wait_ge(q_hi, n + 1)
                    rows = q_st[64:EXT, g, h * HT:(h + 1) * HT]
                    dve.scalar_tensor_tensor(out=rows, in0=bank[Q_BANKS[h][g]][64:EXT, :],
                                             scalar=bias_cols[64:EXT, RQ + g:RQ + g + 1],
                                             in1=rows.bitcast(F32), op0=ALU.add,
                                             op1=ALU.subtract).then_inc(q_lo, 1)

            def maxima(b, t):
                for half in range(2):
                    n = 2 * (TB * b + t) + half
                    dve.wait_ge(s_done, n + 1)
                    dve.tensor_reduce(nmax[:, TB * b + t, 8 * half:8 * half + 8],
                                      bank[half][:].rearrange("p (a k) -> p a k", k=SK), AX.X, ALU.max,
                                      negate=True).then_inc(max_read, 1)

            def max_parts(b):
                dve.wait_ge(max_read, 2 * TB * (b + 1))
                t = slice(TB * b, TB * (b + 1))
                rows = nmax[:, t, :].rearrange("p t (g j) -> p t g j", g=G)
                link(dve.tensor_copy(nm_cols[:, t, :, 1:1 + GH], rows))
                dve.tensor_tensor(nm_cols[:, t, :, 1 + GH:1 + 2 * GH], rows, nm_cols[:, t, :, 1:1 + GH].bitcast(F32),
                                  ALU.subtract).then_inc(nm_ready, 1)

            def normed_values(b):
                dve.wait_ge(sums_ready, 2 * (b + 1))
                link(dve.reciprocal(sumT[:], sumT[:]))
                for gg in range(2):
                    dve.tensor_tensor(attnT[PV[gg], b % 2, :], bank[4 + b % 2][PV[gg], gg * S:(gg + 1) * S], sumT[PV[gg], :],
                                      ALU.mult).then_inc(attn_ready, 1)

            def residual(b):
                dve.wait_ge(proj_done, b + 1)
                dve.wait_ge(xb_ready, b // BH + 1)
                t = slice(TB * b, TB * (b + 1))
                dve.tensor_tensor(x1[:, t, :], bank[7][:, 0:TB * D].rearrange("p (t d) -> p t d", t=TB),
                                  xb[:, t, :], ALU.add).then_inc(x1_ready, 1)
                dve.wait_ge(x1_ready, b + 1)
                norm_stats(x1, mv2, TB * b, TB * (b + 1)).then_inc(var2, 1)

            def second_norm(b):
                dve.wait_ge(rstd2_ready, b + 1)
                for t in range(TB * b, TB * (b + 1)):
                    normalise(x2n, x1, mv2, rstd2, t).then_inc(x2n_ready, 1)

            def x2_lo(b):
                dve.wait_ge(x2hi_ready, b + 1)
                dve.wait_ge(x2T_ready, b + 1)
                c = slice(b * S, (b + 1) * S)
                dve.tensor_tensor(x2T_lo[:, c], x2T[:, c], x2T_hi[:, c].bitcast(F32), ALU.subtract).then_inc(x2lo_ready, 1)

            def logits(h):
                t = slice(h * TH, (h + 1) * TH)
                dve.wait_ge(gate_done, BH * (h + 1))
                dve.wait_ge(ld_bg, 16)
                link(dve.tensor_tensor(logit[:, t, :], bank[6][:, S + h * TH * E:S + (h + 1) * TH * E].rearrange("p (t e) -> p t e", t=TH),
                                       bg_bc[:].unsqueeze(1).to_broadcast([P, TH, E]), ALU.add))
                link(dve.tensor_reduce(lmax[:, t], logit[:, t, :], AX.X, ALU.max))
                dve.tensor_tensor(logit[:, t, :], logit[:, t, :], lmax[:, t].unsqueeze(2).to_broadcast([P, TH, E]),
                                  ALU.subtract).then_inc(logit_ready, 1)

            def select(h):
                t = slice(h * TH, (h + 1) * TH)
                bc = lambda a: a.to_broadcast([P, TH, E])
                dve.wait_ge(prob_exp, h + 1)
                link(dve.tensor_reduce(psumv[:, t], prob[:, t, :], AX.X, ALU.add))
                link(dve.reciprocal(psumv[:, t], psumv[:, t]))
                link(dve.tensor_tensor(prob[:, t, :], prob[:, t, :], bc(psumv[:, t].unsqueeze(2)), ALU.mult))
                for u in range(h * TH, (h + 1) * TH):
                    count(dve.max(top[:, u, :], prob[:, u, :]))
                dve.wait_ge(dve_step, steps[0])
                for u in range(h * TH, (h + 1) * TH):
                    count(dve.max_index(top_at[:, u, :], top[:, u, :], prob[:, u, :]))
                dve.wait_ge(dve_step, steps[0])
                count(dve.tensor_tensor(first[:, t, :], col_e[:].unsqueeze(1).to_broadcast([P, TH, E]),
                                        bc(top_at[:, t, 0:1]), ALU.is_equal))
                count(dve.tensor_tensor(second[:, t, :], col_e[:].unsqueeze(1).to_broadcast([P, TH, E]),
                                        bc(top_at[:, t, 1:2]), ALU.is_equal))
                link(dve.tensor_tensor(norm[:, t], top[:, t, 0], top[:, t, 1], ALU.add))
                count(dve.tensor_tensor(first[:, t, :], first[:, t, :], second[:, t, :], ALU.add))
                link(dve.tensor_scalar(norm[:, t], norm[:, t], 1e-8, None, ALU.add))
                count(dve.reciprocal(norm[:, t], norm[:, t]))
                link(dve.tensor_tensor(sel[:, t, :], prob[:, t, :], first[:, t, :], ALU.mult))
                link(dve.tensor_tensor(sel[:, t, :], sel[:, t, :], bc(norm[:, t].unsqueeze(2)), ALU.mult))
                link(dve.tensor_copy(sel_parts[:, t, 0:E], sel[:, t, :]))
                dve.tensor_tensor(sel_parts[:, t, E:2 * E], sel[:, t, :], sel_parts[:, t, 0:E].bitcast(F32),
                                  ALU.subtract).then_inc(sel_ready, 1)

            q_lo_of(0)
            first_norm(1)
            dve.wait_ge(fill_ready, 1)
            for t in range(TB):
                maxima(0, t)
            max_parts(0)
            dve.wait_ge(ident_ready, 1)
            dve.tensor_tensor(pick[:], ident[0:2 * E, 0:E], ident[0:2 * E, E:2 * E], ALU.add).then_inc(pick_ready, 1)
            q_lo_of(1)
            dve.wait_ge(v_done, 1)
            dve.wait_ge(ld_bv, 16)
            dve.wait_ge(v_filled, V_FILLS)
            for j in range(2):
                rows = slice(SK * j, SK * (j + 1))
                cols = slice(HD * j, HD * (j + 1))
                for b in range(B):
                    dve.tensor_tensor(v_diag[rows, b, :, cols],
                                      bank[5][rows, b * D:(b + 1) * D].rearrange("p (r w) -> p r w", r=PR)[:, :, cols],
                                      bv_bc[rows, :].rearrange("p (r w) -> p r w", r=PR)[:, :, cols],
                                      ALU.add).then_inc(v_ready, 1)
            dve.wait_ge(pick_ready, 1)
            for e in range(2):
                stage(e, e)
            for b in range(B):
                if b + 1 < B:
                    maxima(b + 1, 0)
                if b >= 2:
                    second_norm(b - 2)
                if b + 1 < B:
                    maxima(b + 1, 1)
                    max_parts(b + 1)
                if b >= 1:
                    normed_values(b - 1)
                if b >= 2:
                    x2_lo(b - 2)
                if b == B - 1:
                    logits(0)
                    select(0)
                if b >= 1:
                    residual(b - 1)
            second_norm(B - 2)
            normed_values(B - 1)
            residual(B - 1)
            x2_lo(B - 2)
            second_norm(B - 1)
            x2_lo(B - 1)
            logits(1)
            select(1)

            def scale(i, uu):
                unit = 2 * NH * i + uu
                e = 2 * i + uu // NH
                c = uu % NH
                dve.wait_ge(down_done, HC * (unit + 1))
                dve.wait_ge(sel_copied, unit + 1)
                after(dve, y_added, unit - 1)
                bias = bias_cols[:, R2 + e:R2 + e + 1] if known(i) else bias_cols[:, bass.ds(R2 + e, 1)]
                dve.scalar_tensor_tensor(out=part[:, c, :], in0=bank[4 + c][:], scalar=bias, in1=sel_now[:, c, :],
                                         op0=ALU.add, op1=ALU.mult).then_inc(y_scaled, 1)

            def body(i):
                for jj in range(PER):
                    j = i * PER + jj
                    dve.wait_ge(gelu_done, j + 1)
                    dve.tensor_copy(hid_hi[:, jj % RING, :], hid[:, jj % RING, :]).then_inc(hid_split, 1)
                    if jj % HC < HC - 1:
                        dve.wait_ge(hid_split, j + 1)
                        hid_low(dve, jj).then_inc(lo_dve, 1)
                    e = 2 * i + jj // (2 * HC) + 1
                    if jj % (2 * HC) in (4, 6) and not (known(i) and not 2 <= e < E):
                        which = jj % (2 * HC) // 2 - 2
                        dve.wait_ge(down_done, 2 * HC * (e - 1))
                        dve.tensor_copy(w_hi[:, 1 - jj // (2 * HC), which, :], weight(e, which)).then_inc(wsplit_hi, 1)
                        if which == 0:
                            dve.wait_ge(gelu_done, 2 * HC * (e - 1))
                            stage(e, 1 - jj // (2 * HC))
                    if jj % HC == 0:
                        uu = jj // HC - 2
                        if uu >= 0:
                            scale(i, uu)
                        elif not known(i) or i > 0:
                            scale(i - 1, 2 * NH + uu)

            iterations(dve, body)
            for c in range(NH):
                scale(ITER - 1, NH + c)
            for h in range(NH):
                dve.wait_ge(outT_done, h + 1)
                t = slice(h * TH, (h + 1) * TH)
                dve.tensor_tensor(y_out[:, t, :], bank[6 + h][:].rearrange("p (t d) -> p t d", t=TH), x1[:, t, :],
                                  ALU.add).then_inc(out_ready, 1)

        @block.tensor
        def _(pe):
            pe.wait_ge(ident_ready, 1)
            for _ in range(WARM_UP):
                pe.transpose(bank[0][:, 0:P], ident[:], ident[:])
            pe.wait_ge(ld_ctx, 16)
            for c in range(KEYS // P):
                ins = pe.transpose(bank[6][:, c * P:(c + 1) * P], ctx_sb[:, c, :], ident[:])
            ins.then_inc(ctxT_done, 1)
            pe.wait_ge(ctxT_ready, 2)
            pe.wait_ge(rep_ready, 1)
            for g in range(G):
                pe.matmul(k_bank(g, 0, EXT), wk_rep[:, g, :, :].rearrange("p a c -> p (a c)"), ctxT[:, :, 0, :],
                          start=True, stop=True).then_inc(k_done, 1)
            pe.wait_ge(ld_bias, 16 * 4)
            pe.transpose(bank[7][:, 0:NR], bias_rows[:], ident[0:NR, 0:NR]).then_inc(biasT_done, 1)

            def turn_x(h):
                pe.wait_ge(xn_ready, TH * (h + 1))
                if h == 0:
                    pe.wait_ge(bias_ready, 1)
                else:
                    pe.wait_ge(xnT_ready, 1)
                for t in range(TH):
                    ins = pe.transpose(bank[7][:, t * P:(t + 1) * P], xn[:, h * TH + t, :], ident[:])
                ins.then_inc(xnT_done, 1)

            def queries(h, groups):
                pe.wait_ge(xnT_ready, h + 1)
                pe.wait_ge(rep_ready, 3)
                for g in groups:
                    if h == 0 and g >= 2:
                        pe.wait_ge(k_lo, g - 1)
                    pe.matmul(bank[Q_BANKS[h][g]][0:EXT + 1, :], wq_rep[:, g, :], xnT[:, h, :],
                              start=True, stop=True).then_inc(q_done, 1)

            def scores(b, n):
                t, half = TB * b + n // 2, n % 2
                at = 2 * TB * b + n
                if at >= 2:
                    pe.wait_ge(max_read, at - 1)
                for gg in range(2):
                    g = 2 * half + gg
                    ins = pe.matmul(bank[half][:, gg * 256:(gg + 1) * 256], q_st[0:EXT + 1, g, t * P:(t + 1) * P],
                                    k_blk[0:EXT + 1, g, b, :, :].rearrange("p j k -> p (j k)"), start=True, stop=True)
                ins.then_inc(s_done, 1)

            def max_rows(b):
                pe.wait_ge(nm_ready, b + 1)
                if b:
                    after(pe, x1_ready, b - 2)
                else:
                    pe.wait_ge(xnT_ready, 2)
                for t in range(TB):
                    ins = pe.transpose(bank[7][:, t * P:(t + 1) * P],
                                       nm_cols[:, TB * b + t, :, :].rearrange("p g r -> p (g r)").bitcast(F32), ident[:])
                ins.then_inc(nmT_done, 1)

            def scoresT(b, n):
                m = PR // 2 * b + n
                if m < 2:
                    pe.wait_ge(q_lo, G + m + 1)
                else:
                    pe.wait_ge(exp_done, m - 1)
                for k in range(2):
                    pair = 2 * n + k
                    g, j = pair // 2, 2 * (pair % 2)
                    ins = pe.matmul(bank[2 + n % 2][:, k * S:(k + 1) * S], k_blk[:, g, b, j:j + 2, :].rearrange("p j k -> p (j k)"),
                                    q_st[:, g, b * S:(b + 1) * S], start=True, stop=True)
                ins.then_inc(st_done, 1)

            def values(b, gg):
                if gg == 0:
                    if b >= 2:
                        pe.wait_ge(attn_ready, 2 * (b - 1))
                    else:
                        pe.wait_ge(q_lo, G + 3)
                        pe.wait_ge(v_ready, 2 * B)
                for pair in range(PR // 2 * gg, PR // 2 * (gg + 1)):
                    pe.wait_ge(exp_done, PR // 2 * b + pair // 2 + 1)
                    ins = pe.matmul(bank[4 + b % 2][:, gg * S:(gg + 1) * S], v_blk[:, b, pair * P:(pair + 1) * P],
                                    probsT[:, b % 2, pair, :], start=(pair % 4 == 0), stop=(pair % 4 == 3))
                if gg:
                    ins.then_inc(pv_done, 1)

            def project(b):
                pe.wait_ge(attn_ready, 2 * (b + 1))
                pe.wait_ge(ld_wo, 16)
                pe.wait_ge(nmT_ready, G * min(b + 3, B))
                for t in range(TB):
                    ins = pe.matmul(bank[7][:, t * D:(t + 1) * D], attnT[:, b % 2, t * P:(t + 1) * P], wo_sb[:],
                                    start=True, stop=True)
                ins.then_inc(proj_done, 1)

            def turn_x2(b):
                pe.wait_ge(x2n_ready, TB * (b + 1))
                if b:
                    pe.wait_ge(x2T_ready, b)
                    if b == BH:
                        pe.wait_ge(logit_ready, 1)
                else:
                    pe.wait_ge(q_lo, 2 * G)
                for t in range(TB):
                    ins = pe.transpose(bank[6][:, t * P:(t + 1) * P], x2n[:, TB * b + t, :], ident[:])
                ins.then_inc(x2T_done, 1)

            def gates(b):
                pe.wait_ge(x2T_ready, b + 1)
                pe.wait_ge(ld_wg, 16)
                for t in range(TB * b, TB * (b + 1)):
                    at = S + t * E
                    ins = pe.matmul(bank[6][:, at:at + E], x2T[:, t * P:(t + 1) * P], wg_sb[:], start=True, stop=True)
                ins.then_inc(gate_done, 1)

            turn_x(0)
            queries(0, range(G))
            for b in range(B):
                ins = pe.matmul(bank[5][:, b * D:(b + 1) * D], ctxT[:, b, :, :].rearrange("p a k -> p (a k)"),
                                wkv_sb[:, D:2 * D], start=True, stop=True)
            ins.then_inc(v_done, 1)
            pe.wait_ge(q_lo, G)
            pe.wait_ge(k_blk_dve, 2 * GH)
            pe.wait_ge(k_blk_act, 2 * GH)
            pe.wait_ge(ext_ready, 1)
            pe.wait_ge(ext_copied, 16)
            for n in range(2 * TB):
                scores(0, n)
                if n == 1:
                    turn_x(1)
            queries(1, (0, 1))
            pe.wait_ge(fill_ready, 1)
            max_rows(0)
            queries(1, (2, 3))
            for b in range(B):
                pe.wait_ge(nmT_ready, G * (b + 1))
                if b + 1 == BH:
                    pe.wait_ge(q_lo, 2 * G)
                for n in range(PR // 2):
                    scoresT(b, n)
                    if b + 1 < B:
                        scores(b + 1, n)
                if b >= 2:
                    turn_x2(b - 2)
                values(b, 0)
                if b + 1 < B:
                    max_rows(b + 1)
                if b >= 2:
                    gates(b - 2)
                values(b, 1)
                if b >= 1:
                    project(b - 1)

            def up(i, jj):
                j = i * PER + jj
                slot = jj // (2 * HC)
                c = jj // HC % NH
                hc = jj % HC
                if jj % (2 * HC) == 0:
                    pe.wait_ge(wsplit, 2 * (2 * i + slot) + 1)
                if known(i) and i == 0 and jj in (0, HC):
                    pe.wait_ge(x2hi_ready, BH * (c + 1))
                    pe.wait_ge(x2lo_ready, BH * (c + 1))
                after(pe, gelu_done, j - RING + 1)
                w = slice(hc * P, (hc + 1) * P)
                q = slice(c * HT, (c + 1) * HT)
                for n, (a, m) in enumerate(((w_hi, x2T_hi), (w_hi, x2T_lo), (w_lo, x2T_hi))):
                    ins = pe.matmul(bank[jj % RING][:], a[:, slot, 0, w], m[:, q], start=(n == 0), stop=(n == 2))
                ins.then_inc(up_done, 1)

            def down(i, jj):
                j = i * PER + jj
                slot = jj // (2 * HC)
                c = jj // HC % NH
                hc = jj % HC
                if jj % (2 * HC) == 0:
                    pe.wait_ge(wsplit, 2 * (2 * i + slot) + 2)
                if hc == 0:
                    after(pe, y_scaled, 2 * NH * i + jj // HC - 1)
                    if known(i) and i == 0 and slot == 0:
                        pe.wait_ge(selT_ready, c + 1)
                    pe.wait_ge(staged, 2 * (2 * i + slot + 1))
                    pe.matmul(bank[6 + c][:], pick_now[:, slot, :], selT[:, c, :], start=True, stop=True).then_inc(bc_done, 1)
                wait_lo(pe, i * 2 * NH + jj // HC, hc)
                w = slice(hc * D, (hc + 1) * D)
                for n, (a, m) in enumerate(((w_hi, hid_hi), (w_hi, hid_lo), (w_lo, hid_hi))):
                    ins = pe.matmul(bank[4 + c][:], a[:, slot, 1, w], m[:, jj % RING, :],
                                    start=(hc == 0 and n == 0), stop=(hc == HC - 1 and n == 2))
                ins.then_inc(down_done, 1)

            def turn_sel(h):
                pe.wait_ge(sel_ready, h + 1)
                for t in range(TH):
                    ins = pe.transpose(bank[6 - h][0:2 * E, t * P:(t + 1) * P],
                                       sel_parts[:, h * TH + t, :].bitcast(F32), ident[:])
                ins.then_inc(selT_done, 1)

            pe.wait_ge(exp_done, PR // 2 * B)
            turn_x2(B - 2)
            up(0, 0)
            gates(B - 2)
            up(0, 1)
            project(B - 1)
            up(0, 2)
            up(0, 3)
            turn_x2(B - 1)
            gates(B - 1)
            pe.wait_ge(logit_ready, NH)
            turn_sel(0)
            turn_sel(1)

            def body(i):
                for jj in range(PER):
                    down(i, jj)
                    if jj + AHEAD < PER:
                        up(i, jj + AHEAD)
                    elif not known(i) or i < ITER - 1:
                        up(i + 1, jj + AHEAD - PER)

            iterations(pe, body)
            for h in range(NH):
                pe.wait_ge(y_added, NH * (E - 1) + h + 1)
                for t in range(TH):
                    ins = pe.transpose(bank[6 + h][:, t * P:(t + 1) * P], acc[:, h, t * P:(t + 1) * P], ident[:])
                ins.then_inc(outT_done, 1)

    return nc


INS = ["x", "ctx_1024", "mask_BxS2_bk0", "L0_xattn_Wq", "L0_xattn_bq", "L0_xattn_Wkv", "L0_xattn_bkv",
       "L0_xattn_Wo", "L0_xattn_bo", "L0_ffn_Wg", "L0_ffn_bg", "L0_ffn_W1", "L0_ffn_b1", "L0_ffn_W2", "L0_ffn_b2"]


def kernel(**inputs):
    import numpy as np
    import concourse.bacc as bacc
    from concourse.bass_utils import run_bass_kernel_spmd

    nc = bacc.Bacc("TRN2", target_bir_lowering=False, num_devices=1)
    arrays, args = {}, []
    for name in INS:
        a = np.ascontiguousarray(inputs[name])
        arrays[f"in_{name}"] = a
        args.append(nc.dram_tensor(f"in_{name}", a.shape, mybir.dt.from_np(a.dtype), kind="ExternalInput").ap())
    args.append(nc.dram_tensor("out_y", arrays["in_x"].shape, F32, kind="ExternalOutput").ap())
    build(nc, *args)
    r = run_bass_kernel_spmd(nc, [arrays], core_ids=[0])
    return r.results[0]["out_y"]
```

```python
from contextlib import ExitStack

import concourse.bass as bass
from concourse import mybir

F32 = mybir.dt.float32
F32R = mybir.dt.float32r
U8 = mybir.dt.uint8
I32 = mybir.dt.int32
U32 = mybir.dt.uint32
ALU = mybir.AluOpType
ACT = mybir.ActivationFunctionType
AX = mybir.AxisListType

P = 128
EPS = 1e-5
MASKED = -1e30
HEADS = 16


def build(nc, x, ctx_in, mask, Wq, bq, Wkv, bkv, Wo, bo, Wg, bg, W1, b1, W2, b2, out):
    B, S, D = x.shape
    SK = ctx_in.shape[1]
    E, _, HID = W1.shape
    T = B * S // P
    TB = S // P
    NH = 2
    TH = T // NH
    HT = TH * P
    BH = B // NH
    HC = HID // P
    HD = D // HEADS
    SCALE = float(HD) ** -0.5
    G = 4
    GH = HEADS // G
    PR = HEADS // 2
    KEYS = B * SK
    EXT = 96
    HALF = P // 2
    VS = P + 2 * HD
    assert D == P and GH * HD == 32 and 2 * SK == P and TB == 2 and HT == 512 and KEYS == 256

    with ExitStack() as stack:
        def sb(name, shape, dt=F32):
            return stack.enter_context(nc.sbuf_tensor(name, shape, dt))

        def sem(name):
            return stack.enter_context(nc.semaphore(name))

        bank = [stack.enter_context(nc.psum_tensor(f"bank{i}", [P, 512], F32)) for i in range(8)]

        x_sb = sb("x_sb", [P, T, D])
        ctx_sb = sb("ctx_sb", [P, KEYS // P, D])
        wq_sb = sb("wq_sb", [P, D])
        wkv_sb = sb("wkv_sb", [P, 2 * D])
        wo_sb = sb("wo_sb", [P, D])
        wg_sb = sb("wg_sb", [P, E])
        w1_sb = sb("w1_sb", [P, E, HID])
        w2_sb = sb("w2_sb", [P, E, HC * D])
        NB1 = E * HC
        R2, RQ, RK, NR = NB1, NB1 + E, NB1 + E + G, NB1 + E + 2 * G
        bias_rows = sb("bias_rows", [NR, P])
        warm = sb("warm", [P, 1])
        bias_cols = sb("bias_cols", [P, NR])
        bv_bc = sb("bv_bc", [P, D])
        bo_bc = sb("bo_bc", [P, D])
        bg_bc = sb("bg_bc", [P, E])
        mask_row = sb("mask_row", [P, KEYS], U8)

        mask_add = sb("mask_add", [P, KEYS])

        ident = sb("ident", [P, P])
        part_i = sb("part_i", [P, GH], I32)
        head_of = sb("head_of", [P, GH], I32)
        col_j = sb("col_j", [P, GH], I32)
        own_head = sb("own_head", [P, GH])
        minus_half = sb("minus_half", [P, T])
        col_e = sb("col_e", [P, E], I32)
        pick = sb("pick", [2 * E, E])

        wq_rep = sb("wq_rep", [P, G, EXT + 1])
        wk_rep = sb("wk_rep", [P, G, 3, 32])
        ctxT = sb("ctxT", [P, B, 2, SK])
        k_mix = sb("k_mix", [EXT, G, KEYS], F32R)
        k_blk = sb("k_blk", [P, G, B, GH, SK], F32R)
        v_blk = sb("v_blk", [P, B, PR * VS])
        stats = sb("stats", [P, T, 6])
        mv1 = sb("mv1", [P, T, 2])
        rstd1 = sb("rstd1", [P, T])
        xn = sb("xn", [P, T, D])
        xnT = sb("xnT", [P, NH, HT])
        q_st = sb("q_st", [P, G, T * P], F32R)
        nmax = sb("nmax", [P, T, HEADS])
        nm_cols = sb("nm_cols", [P, T, G, 32], F32R)
        probs_mem = sb("probs_mem", [P, 2 * PR * S])
        probsT = probs_mem[:].rearrange("p (r a q) -> p r a q", r=2, a=PR)
        ext_sel = probs_mem[:, 0:GH * KEYS].rearrange("p (b j k) -> p b j k", b=B, j=GH)
        sumT = sb("sumT", [P, S])
        attnT = sb("attnT", [P, 2, S])
        xb = sb("xb", [P, T, D])
        x1 = sb("x1", [P, T, D])

        mv2 = sb("mv2", [P, T, 2])
        rstd2 = sb("rstd2", [P, T])
        x2n = xn
        x2T = xnT[:].rearrange("p h q -> p (h q)")
        x2T_hi = sb("x2T_hi", [P, T * P], F32R)
        x2T_lo = sb("x2T_lo", [P, T * P], F32R)
        logit = sb("logit", [P, T, E])
        lmax = sb("lmax", [P, T])
        prob = sb("prob", [P, T, E])
        psumv = sb("psumv", [P, T])
        top = sb("top", [P, T, E])
        top_at = sb("top_at", [P, T, E], U32)
        first = sb("first", [P, T, E])
        second = sb("second", [P, T, E])
        norm = sb("norm", [P, T])
        sel = sb("sel", [P, T, E])
        sel_parts = sb("sel_parts", [P, T, 2 * E], F32R)
        selT = sb("selT", [2 * E, NH, HT], F32R)

        w_hi = sb("w_hi", [P, 2, 2, HID], F32R)
        w_lo = sb("w_lo", [P, 2, 2, HID], F32R)
        RING = 4
        hid = probs_mem[:, 0:RING * HT].rearrange("p (r q) -> p r q", r=RING)
        part = probs_mem[:, RING * HT:(RING + 2) * HT].rearrange("p (r q) -> p r q", r=2)
        k_mem = k_blk[:].rearrange("p g b j k -> p (g b j k)")
        hid_hi = k_mem[:, 0:RING * HT].rearrange("p (r q) -> p r q", r=RING)
        hid_lo = k_mem[:, RING * HT:2 * RING * HT].rearrange("p (r q) -> p r q", r=RING)
        sel_now = sb("sel_now", [P, NH, HT])
        acc = sb("acc", [P, NH, HT])
        b1_now = sb("b1_now", [P, 2, HC])
        pick_now = sb("pick_now", [2 * E, 2, P], F32R)
        y_out = x_sb

        ld_x = [sem(f"ld_x{h}") for h in range(NH)]
        ld_ctx, ld_wq, ld_wkv, ld_wo, ld_wg = (sem(n) for n in ("ld_ctx", "ld_wq", "ld_wkv", "ld_wo", "ld_wg"))
        ld_w = [sem(f"ld_w{e}") for e in range(E)]
        ld_bias, ld_bv, ld_bo, ld_bg, ld_mask = (sem(n) for n in ("ld_bias", "ld_bv", "ld_bo", "ld_bg", "ld_mask"))
        stored = sem("stored")
        pool_step = sem("pool_step")
        half_ready = sem("half_ready")
        zeroed = sem("zeroed")
        ident_ready = sem("ident_ready")
        pick_ready = sem("pick_ready")
        index_ready = sem("index_ready")
        fill_ready = sem("fill_ready")
        ext_ready = sem("ext_ready")
        ext_copied = sem("ext_copied")
        xb_ready = sem("xb_ready")
        dve_step = sem("dve_step")
        rep_ready = sem("rep_ready")
        ones_ready = sem("ones_ready")
        own_ready = sem("own_ready")
        biasT_done, bias_ready = sem("biasT_done"), sem("bias_ready")
        ctxT_done, ctxT_ready = sem("ctxT_done"), sem("ctxT_ready")
        k_done, k_hi, k_lo = (sem(n) for n in ("k_done", "k_hi", "k_lo"))
        k_blk_dve, k_blk_pool, k_blk_act = sem("k_blk_dve"), sem("k_blk_pool"), sem("k_blk_act")
        v_cleared, v_filled, v_done, v_ready = sem("v_cleared"), sem("v_filled"), sem("v_done"), sem("v_ready")
        var1, rstd1_ready, xn_ready = sem("var1"), sem("rstd1_ready"), sem("xn_ready")
        xnT_done, xnT_ready = sem("xnT_done"), sem("xnT_ready")
        q_done, q_hi, q_lo = sem("q_done"), sem("q_hi"), sem("q_lo")
        s_done, max_read, nm_ready = sem("s_done"), sem("max_read"), sem("nm_ready")
        nmT_done, nmT_ready = sem("nmT_done"), sem("nmT_ready")
        st_done, exp_done = sem("st_done"), sem("exp_done")
        pv_done, sums_ready, attn_ready = sem("pv_done"), sem("sums_ready"), sem("attn_ready")
        proj_done, x1_ready = sem("proj_done"), sem("x1_ready")
        var2, rstd2_ready, x2n_ready = sem("var2"), sem("rstd2_ready"), sem("x2n_ready")
        x2T_done, x2T_ready, x2hi_ready, x2lo_ready = (sem(n) for n in ("x2T_done", "x2T_ready", "x2hi_ready", "x2lo_ready"))
        gate_done, logit_ready, prob_exp, sel_ready = (sem(n) for n in ("gate_done", "logit_ready", "prob_exp", "sel_ready"))
        selT_done, selT_ready = sem("selT_done"), sem("selT_ready")
        acc_zero = sem("acc_zero")
        wsplit_hi = sem("wsplit_hi")
        wsplit = sem("wsplit")
        up_done, gelu_done = sem("up_done"), sem("gelu_done")
        staged = sem("staged")
        hid_split, lo_dve, lo_pool, down_done = (sem(n) for n in ("hid_split", "lo_dve", "lo_pool", "down_done"))
        bc_done, sel_copied = sem("bc_done"), sem("sel_copied")
        y_scaled, y_added = sem("y_scaled"), sem("y_added")
        outT_done, out_ready = sem("outT_done"), sem("out_ready")

        x_t = x.rearrange("b (t p) d -> p (b t) d", p=P)
        out_t = out.rearrange("b (t p) d -> p (b t) d", p=P)

        block = stack.enter_context(nc.Block())

        PER = 2 * NH * HC
        ITER = E // 2
        def unit_of(uu):
            return uu % 2, uu // 2

        AHEAD = RING
        SPLITS = {0: (1, 0), 3 * HC: (0, 0), HC - 1: (1, 1), 4 * HC - 1: (0, 1)}
        known = lambda v: isinstance(v, int)

        def k_bank(g, lo, hi):
            return bank[(2, 3, 4, 6)[g]][lo:hi, 0:KEYS]

        def st_bank(b, n):
            return (2, 3, 0, 1)[n] if b == B - 1 else 2 + n % 2

        def x2_bank(b):
            return 6 if b < BH else 7

        K_ORDER = (2, 3, 0, 1)
        Q_BANKS = ((0, 1, 4, 6), (5, 6, 5, 6))
        v_diag = v_blk[:].rearrange("p b (r w) -> p b r w", r=PR)
        V_FILLS = 5
        PV = (slice(0, HALF), slice(HALF, P))
        PS = (slice(HALF, P), slice(0, HALF))

        def after(eng, s, value):
            if not known(value) or value > 0:
                eng.wait_ge(s, value)

        def last_chunk(i, jj):
            return known(i) and i == ITER - 1 and jj == PER - 1

        def wait_lo(eng, unit, hc):
            if hc == HC - 1 and not (known(unit) and unit == NH * E - 1):
                after(eng, lo_pool, unit + 1)
            else:
                after(eng, lo_dve, (HC - 1) * unit + hc + 1)

        def hid_low(eng, jj):
            return eng.tensor_tensor(hid_lo[:, jj % RING, :], hid[:, jj % RING, :],
                                     hid_hi[:, jj % RING, :].bitcast(F32), ALU.subtract)

        def weight(e, which):
            w = (w1_sb, w2_sb)[which]
            return w[:, e, :] if known(e) else w[:, bass.ds(e, 1), :].rearrange("p a n -> p (a n)")

        def iterations(eng, body):
            body(0)
            with eng.Fori(1, ITER - 1) as i:
                body(i)
            body(ITER - 1)

        @block.sync
        def _(sp):
            sp.dma_start(x_sb[:, 0:TH, :], x_t[:, 0:TH, :]).then_inc(ld_x[0], 16)
            sp.dma_start(wkv_sb[:], Wkv).then_inc(ld_wkv, 16)
            sp.dma_start(wq_sb[:], Wq).then_inc(ld_wq, 16)
            sp.dma_start(x_sb[:, TH:T, :], x_t[:, TH:T, :]).then_inc(ld_x[1], 16)
            sp.wait_ge(zeroed, 1)
            sp.dma_start(mask_row[EXT:EXT + 1, :],
                         mask.rearrange("(a b) k -> a (b k)", a=1)).then_inc(ld_mask, 16)
            sp.dma_start(bv_bc[:], bkv[D:2 * D].rearrange("(a d) -> a d", a=1).to_broadcast([P, D])).then_inc(ld_bv, 16)
            sp.dma_start(wo_sb[:], Wo).then_inc(ld_wo, 16)
            sp.dma_start(bo_bc[:], bo.rearrange("(a d) -> a d", a=1).to_broadcast([P, D])).then_inc(ld_bo, 16)
            sp.dma_start(wg_sb[:], Wg).then_inc(ld_wg, 16)
            sp.dma_start(bg_bc[:], bg.rearrange("(a d) -> a d", a=1).to_broadcast([P, E])).then_inc(ld_bg, 16)
            sp.wait_ge(ext_copied, 16)
            for e in range(E):
                sp.dma_start(w1_sb[:, e, :], W1[e]).then_inc(ld_w[e], 16)
                sp.dma_start(w2_sb[:, e, :].rearrange("p (c f) -> p c f", c=HC),
                             W2[e].rearrange("(c p) f -> p c f", p=P)).then_inc(ld_w[e], 16)
            for h in range(NH):
                sp.wait_ge(out_ready, h + 1)
                sp.dma_start(out_t[:, h * TH:(h + 1) * TH, :], y_out[:, h * TH:(h + 1) * TH, :]).then_inc(stored, 16)
            sp.wait_ge(stored, 16 * NH)

        @block.gpsimd
        def _(pool):
            steps = [0]

            def link(ins):
                steps[0] += 1
                ins.then_inc(pool_step, 1)
                pool.wait_ge(pool_step, steps[0])

            pool.memset(minus_half[:], -0.5).then_inc(half_ready, 1)
            pool.wait_ge(half_ready, 1)
            pool.memset(mask_row[EXT:P, :], 0).then_inc(zeroed, 1)
            pool.wait_ge(zeroed, 1)
            link(pool.memset(ident[:], 0.0))
            pool.affine_select(out=ident[:], in_=ident[:], compare_op=ALU.not_equal, fill=1.0, base=0,
                               pattern=[[-1, P]], channel_multiplier=1).then_inc(ident_ready, 1)
            pool.iota(part_i[:], pattern=[[0, GH]], base=0, channel_multiplier=1).then_inc(index_ready, 1)
            pool.iota(col_j[:], pattern=[[1, GH]], base=0, channel_multiplier=0).then_inc(index_ready, 1)
            pool.iota(col_e[:], pattern=[[1, E]], base=0, channel_multiplier=0).then_inc(index_ready, 1)
            pool.wait_ge(index_ready, 3)

            def rstd(mv, rs, lo, hi):
                link(pool.tensor_scalar(rs[:, lo:hi], mv[:, lo:hi, 1], EPS, 1.0, ALU.add, ALU.mult))
                return pool.tensor_tensor(rs[:, lo:hi], rs[:, lo:hi], minus_half[:, lo:hi], ALU.pow)

            ext = ext_sel[EXT:P, :, :, :]
            def own_ones(first_row):
                return pool.affine_select(out=ext, in_=ext, compare_op=ALU.not_equal, fill=1.0, base=-first_row,
                                          pattern=[[0, B], [-1, GH], [0, SK]], channel_multiplier=1)

            link(pool.memset(ext, 0.0))
            link(own_ones(1))
            pool.wait_ge(var1, 1)
            rstd(mv1, rstd1, 0, TH).then_inc(rstd1_ready, 1)
            pool.wait_ge(rstd1_ready, 1)
            link(own_ones(1 + GH))
            pool.wait_ge(ld_mask, 16)
            link(pool.tensor_scalar(mask_add[EXT:P, :], mask_row[EXT:P, :], MASKED, 1.0, ALU.mult, ALU.mult))
            pool.tensor_tensor(k_blk[EXT:P, 0, :, :, :], ext, mask_add[EXT:P, :].rearrange("p (b k) -> p b k", b=B)
                               .unsqueeze(2).to_broadcast([P - EXT, B, GH, SK]), ALU.add).then_inc(ext_ready, 1)
            pool.wait_ge(ext_ready, 1)
            pool.dma_start(k_blk[EXT:P, 1:G, :, :, :].rearrange("p g b j k -> p g (b j k)"),
                           k_blk[EXT:P, 0:1, :, :, :].rearrange("p g b j k -> p g (b j k)")
                           .to_broadcast([P - EXT, G - 1, KEYS * GH])).then_inc(ext_copied, 16)
            pool.wait_ge(k_lo, G)
            pool.wait_ge(own_ready, 1)
            for j in range(GH):
                pool.tensor_scalar(k_blk[0:EXT, 1, :, j, :], k_mix[:, 1, :].rearrange("p (b k) -> p b k", b=B).bitcast(F32),
                                   own_head[0:EXT, j:j + 1], 1.0, ALU.mult, ALU.mult).then_inc(k_blk_pool, 1)
            pool.wait_ge(k_blk_pool, GH)
            pool.wait_ge(var1, 2)
            rstd(mv1, rstd1, TH, T).then_inc(rstd1_ready, 1)
            link(pool.memset(nm_cols[:].bitcast(F32), 0.0))
            pool.memset(nm_cols[:, :, :, 0:1].bitcast(F32), 1.0).then_inc(fill_ready, 1)
            pool.wait_ge(fill_ready, 1)
            pool.memset(v_blk[:, BH:B, :], 0.0).then_inc(v_filled, 1)
            pool.wait_ge(v_cleared, 1)
            fills = 1
            for j in range(2):
                rows = slice(SK * j, SK * (j + 1))
                for r, at in ((0, HALF + HD * j), (PR // 2 - 1, VS - HALF + HD * j)):
                    pool.wait_ge(v_filled, fills)
                    pool.memset(v_diag[rows, :, r:r + PR // 2, at:at + HD], 1.0).then_inc(v_filled, 1)
                    fills += 1
            assert fills == V_FILLS
            pool.wait_ge(v_filled, fills)
            pool.wait_ge(ld_bo, 16)
            for h in range(NH):
                pool.wait_ge(ld_x[h], 16)
                t = slice(h * TH, (h + 1) * TH)
                pool.tensor_tensor(xb[:, t, :], x_sb[:, t, :],
                                   bo_bc[:].unsqueeze(1).to_broadcast([P, TH, D]), ALU.add).then_inc(xb_ready, 1)

            def weight_lo(e, slot, which):
                pool.wait_ge(wsplit_hi, 2 * e + which + 1)
                pool.tensor_tensor(w_lo[:, slot, which, :], weight(e, which), w_hi[:, slot, which, :].bitcast(F32),
                                   ALU.subtract).then_inc(wsplit, 1)

            pool.memset(acc[:], 0.0).then_inc(acc_zero, 1)

            def weights(e):
                pool.wait_ge(ld_w[e], 32)
                for which in range(2):
                    pool.tensor_scalar(w_hi[:, e, which, :], weight(e, which), 1.0, 1.0, ALU.mult, ALU.mult).then_inc(wsplit_hi, 1)
                    weight_lo(e, e, which)

            def second_rstd(b):
                pool.wait_ge(var2, b + 1)
                rstd(mv2, rstd2, TB * b, TB * (b + 1)).then_inc(rstd2_ready, 1)

            def x2_lo(b):
                pool.wait_ge(x2hi_ready, b + 1)
                pool.wait_ge(x2T_ready, b + 1)
                c = slice(b * S, (b + 1) * S)
                pool.tensor_tensor(x2T_lo[:, c], x2T[:, c], x2T_hi[:, c].bitcast(F32), ALU.subtract).then_inc(x2lo_ready, 1)

            weights(0)
            second_rstd(0)
            weights(1)
            for b in range(B):
                if b >= 1:
                    second_rstd(b)
                if b == 1:
                    x2_lo(0)
                if b >= 1:
                    x2_lo(b)
            for e in range(2, E):
                pool.wait_ge(ld_w[e], 32)
            pool.wait_ge(acc_zero, 1)

            def body(i):
                for jj in range(PER):
                    j = i * PER + jj
                    if jj % HC == HC - 1 and not last_chunk(i, jj):
                        pool.wait_ge(hid_split, j + 1)
                        hid_low(pool, jj).then_inc(lo_pool, 1)
                    if jj in SPLITS:
                        slot, which = SPLITS[jj]
                        e = 2 * i + 2 - slot
                        if not (known(i) and not 2 <= e < E):
                            weight_lo(e, slot, which)
                    if jj % HC == 1:
                        unit = 2 * NH * i + jj // HC - 2
                        if not known(unit) or unit >= 0:
                            add(unit, unit_of((jj // HC - 2) % (2 * NH))[1], jj // HC % 2)

            def add(unit, c, r):
                pool.wait_ge(y_scaled, unit + 1)
                after(pool, y_added, unit)
                pool.tensor_tensor(acc[:, c, :], acc[:, c, :], part[:, r, :], ALU.add).then_inc(y_added, 1)

            iterations(pool, body)
            add(NH * E - 2, 1, 0)

        @block.scalar
        def _(act):
            act.dma_start(ctx_sb[:], ctx_in.rearrange("b k d -> (b k) d").rearrange("(t p) d -> p t d", p=P)).then_inc(ld_ctx, 16)
            act.wait_ge(half_ready, 1)
            act.activation(warm[:], minus_half[:, 0:1], ACT.Exp)
            for r, b_in in ((RK, bkv[0:D]), (RQ, bq)):
                act.dma_start(bias_rows[r:r + G, :].rearrange("g (a c) -> g a c", a=4),
                              b_in.rearrange("(g c) -> g c", g=G).unsqueeze(1).to_broadcast([G, 4, 32])).then_inc(ld_bias, 16)
            act.dma_start(bias_rows[0:NB1, :], b1.rearrange("e (c p) -> (e c) p", p=P)).then_inc(ld_bias, 16)
            act.dma_start(bias_rows[R2:R2 + E, :], b2).then_inc(ld_bias, 16)

            act.wait_ge(ctxT_done, 1)
            for c in range(2):
                act.copy(ctxT[:, :, c, :], bank[6][:, 0:KEYS].rearrange("p (b k) -> p b k", b=B)).then_inc(ctxT_ready, 1)
            act.wait_ge(biasT_done, 1)
            act.copy(bias_cols[:], bank[5][:, 0:NR]).then_inc(bias_ready, 1)
            act.wait_ge(bias_ready, 1)

            def keys_hi(n):
                g = K_ORDER[n]
                act.wait_ge(k_done, n + 1)
                act.activation(k_mix[:, g, :], k_bank(g, 0, EXT), ACT.Identity,
                               bias=bias_cols[0:EXT, RK + g:RK + g + 1]).then_inc(k_hi, 1)

            def xnT_of(h):
                act.wait_ge(xnT_done, h + 1)
                act.copy(xnT[:, h, :], bank[7 - h][:]).then_inc(xnT_ready, 1)

            def q_hi_of(h, g):
                act.wait_ge(q_done, G * h + g + 1)
                act.activation(q_st[0:EXT + 1, g, h * HT:(h + 1) * HT], bank[Q_BANKS[h][g]][0:EXT + 1, :], ACT.Identity,
                               bias=bias_cols[0:EXT + 1, RQ + g:RQ + g + 1]).then_inc(q_hi, 1)

            def nm_rows(b):
                act.wait_ge(nmT_done, b + 1)
                for g in range(G):
                    act.copy(q_st[EXT:P, g, b * S:(b + 1) * S], bank[7][32 * g:32 * g + 32, 0:S]).then_inc(nmT_ready, 1)

            def exps(b):
                for n in range(PR // 2):
                    act.wait_ge(st_done, PR // 2 * b + n + 1)
                    if b >= 2 and n == 0:
                        act.wait_ge(pv_done, b - 1)
                    act.activation(probsT[:, b % 2, 2 * n:2 * n + 2, :], bank[st_bank(b, n)][:].rearrange("p (a q) -> p a q", a=2),
                                   ACT.Exp, scale=SCALE).then_inc(exp_done, 1)

            def sums_of(b):
                act.wait_ge(pv_done, b + 1)
                if b:
                    act.wait_ge(attn_ready, 2 * b)
                for gg in range(2):
                    act.copy(sumT[PV[gg], :], bank[4 + b % 2][PS[gg], gg * S:(gg + 1) * S]).then_inc(sums_ready, 1)

            def x2T_of(b):
                act.wait_ge(x2T_done, b + 1)
                act.copy(x2T_hi[:, b * S:(b + 1) * S], bank[x2_bank(b)][:, 0:S]).then_inc(x2hi_ready, 1)
                act.copy(x2T[:, b * S:(b + 1) * S], bank[x2_bank(b)][:, 0:S]).then_inc(x2T_ready, 1)

            def k_blocks(g):
                act.wait_ge(own_ready, 1)
                act.wait_ge(k_lo, K_ORDER.index(g) + 1)
                for j in range(GH):
                    act.activation(k_blk[0:EXT, g, :, j, :], k_mix[:, g, :].rearrange("p (b k) -> p b k", b=B).bitcast(F32),
                                   ACT.Copy, scale=own_head[0:EXT, j:j + 1]).then_inc(k_blk_act, 1)

            keys_hi(0)
            keys_hi(1)
            xnT_of(0)
            keys_hi(2)
            keys_hi(3)
            k_blocks(2)
            act.wait_ge(ones_ready, 1)
            for g in range(G):
                q_hi_of(0, g)
            k_blocks(3)
            nm_rows(0)
            xnT_of(1)

            def gate_exp(h):
                t = slice(h * TH, (h + 1) * TH)
                act.wait_ge(logit_ready, h + 1)
                act.activation(prob[:, t, :], logit[:, t, :], ACT.Exp).then_inc(prob_exp, 1)

            for b in range(B):
                exps(b)
                if b >= 2:
                    x2T_of(b - 2)
                if b == 0:
                    q_hi_of(1, 0)
                    q_hi_of(1, 1)
                if b + 1 < B:
                    nm_rows(b + 1)
                if b == 0:
                    q_hi_of(1, 2)
                    q_hi_of(1, 3)
                if b == B - 1:
                    gate_exp(0)
                sums_of(b)
            x2T_of(B - 2)

            def selT_of(h):
                act.wait_ge(selT_done, h + 1)
                act.copy(selT[:, h, :], bank[6 + h][0:2 * E, :]).then_inc(selT_ready, 1)

            def weights_of_tokens(i, uu):
                unit = 2 * NH * i + uu
                act.wait_ge(bc_done, unit + 1)
                after(act, y_scaled, unit - 1)
                act.copy(sel_now[:, uu % 2, :], bank[6][:]).then_inc(sel_copied, 1)

            def gelu(i, jj):
                j = i * PER + jj
                slot = unit_of(jj // HC)[0]
                if jj % HC == 0:
                    act.wait_ge(staged, 2 * (2 * i + slot) + 1)
                act.wait_ge(up_done, j + 1)
                act.activation(hid[:, jj % RING, :], bank[jj % RING][:], ACT.Gelu_apprx_tanh,
                               bias=b1_now[:, slot, jj % HC:jj % HC + 1]).then_inc(gelu_done, 1)

            def body(i):
                for jj in range(PER):
                    gelu(i, jj)
                    if jj % HC == HC - 1:
                        uu = jj // HC - 1
                        if uu >= 0:
                            weights_of_tokens(i, uu)
                        elif not known(i) or i > 0:
                            weights_of_tokens(i - 1, 2 * NH + uu)
                    if known(i) and i == 0:
                        if jj == 3:
                            x2T_of(B - 1)
                        if jj == 5:
                            selT_of(0)
                        if jj == 6:
                            gate_exp(1)
                        if jj == 11:
                            selT_of(1)

            iterations(act, body)
            weights_of_tokens(ITER - 1, 2 * NH - 1)

        @block.vector
        def _(dve):
            steps = [0]

            def link(ins):
                steps[0] += 1
                ins.then_inc(dve_step, 1)
                dve.wait_ge(dve_step, steps[0])

            def count(ins):
                steps[0] += 1
                ins.then_inc(dve_step, 1)

            def norm_stats(src, mv, lo, hi):
                for t in range(lo, hi):
                    ins = dve.bn_stats(stats[:, t, :], src[:, t, :])
                    count(ins)
                dve.wait_ge(dve_step, steps[0])
                for t in range(lo, hi):
                    ins = dve.bn_aggr(mv[:, t, :], stats[:, t, :])
                return ins

            def normalise(dst, src, mv, rs, t):
                return dve.tensor_scalar(dst[:, t, :], src[:, t, :], mv[:, t, 0:1], rs[:, t:t + 1],
                                         ALU.subtract, ALU.mult)

            def first_stats(h):
                dve.wait_ge(ld_x[h], 16)
                norm_stats(x_sb, mv1, h * TH, (h + 1) * TH).then_inc(var1, 1)

            dve.memset(v_blk[:, 0:BH, :], 0.0).then_inc(v_cleared, 1)

            def first_norm(h):
                dve.wait_ge(rstd1_ready, h + 1)
                for t in range(h * TH, (h + 1) * TH):
                    normalise(xn, x_sb, mv1, rstd1, t).then_inc(xn_ready, 1)

            first_stats(0)
            dve.wait_ge(index_ready, 3)
            link(dve.tensor_scalar(head_of[:], part_i[:], 31, 3, ALU.bitwise_and, ALU.logical_shift_right))
            dve.tensor_tensor(own_head[:], head_of[:], col_j[:], ALU.is_equal).then_inc(own_ready, 1)
            dve.wait_ge(ld_wkv, 16)
            dve.tensor_copy(wk_rep[:], wkv_sb[:, 0:D].rearrange("p (g c) -> p g c", g=G).unsqueeze(2)
                            .to_broadcast([P, G, 3, 32])).then_inc(rep_ready, 1)
            first_norm(0)
            dve.wait_ge(ld_wq, 16)
            dve.memset(wq_rep[:, :, EXT:EXT + 1], 0.0).then_inc(rep_ready, 1)
            dve.tensor_copy(wq_rep[:, :, 0:EXT].rearrange("p g (a c) -> p g a c", a=3), wq_sb[:].rearrange("p (g c) -> p g c", g=G).unsqueeze(2)
                            .to_broadcast([P, G, 3, 32])).then_inc(rep_ready, 1)

            first_stats(1)
            dve.wait_ge(bias_ready, 1)
            dve.memset(bias_cols[EXT:EXT + 1, RQ:RQ + G], 1.0).then_inc(ones_ready, 1)
            dve.wait_ge(own_ready, 1)
            for n, g in enumerate(K_ORDER):
                dve.wait_ge(k_hi, n + 1)
                dve.scalar_tensor_tensor(out=k_mix[32:64, g, :], in0=k_bank(g, 32, 64),
                                         scalar=bias_cols[32:64, RK + g:RK + g + 1],
                                         in1=k_mix[32:64, g, :].bitcast(F32), op0=ALU.add,
                                         op1=ALU.subtract).then_inc(k_lo, 1)
            dve.wait_ge(k_lo, G)
            for j in range(GH):
                dve.tensor_scalar(k_blk[0:EXT, 0, :, j, :], k_mix[:, 0, :].rearrange("p (b k) -> p b k", b=B).bitcast(F32),
                                  own_head[0:EXT, j:j + 1], None, ALU.mult).then_inc(k_blk_dve, 1)

            def stage_b1(e, slot):
                cols = bias_cols[:, e * HC:(e + 1) * HC] if known(e) else bias_cols[:, bass.ds(e * HC, HC)]
                dve.tensor_copy(b1_now[:, slot, :], cols).then_inc(staged, 1)

            def stage_pick(e, slot):
                col = pick[:, e:e + 1] if known(e) else pick[:, bass.ds(e, 1)]
                dve.tensor_copy(pick_now[:, slot, :], col.to_broadcast([2 * E, P])).then_inc(staged, 1)

            def q_lo_of(h, groups):
                for g in groups:
                    n = G * h + g
                    dve.wait_ge(q_hi, n + 1)
                    rows = q_st[64:EXT, g, h * HT:(h + 1) * HT]
                    dve.scalar_tensor_tensor(out=rows, in0=bank[Q_BANKS[h][g]][64:EXT, :],
                                             scalar=bias_cols[64:EXT, RQ + g:RQ + g + 1],
                                             in1=rows.bitcast(F32), op0=ALU.add,
                                             op1=ALU.subtract).then_inc(q_lo, 1)

            def maxima(b, t):
                for half in range(2):
                    n = 2 * (TB * b + t) + half
                    dve.wait_ge(s_done, n + 1)
                    dve.tensor_reduce(nmax[:, TB * b + t, 8 * half:8 * half + 8],
                                      bank[half][:].rearrange("p (a k) -> p a k", k=SK), AX.X, ALU.max,
                                      negate=True).then_inc(max_read, 1)

            def max_parts(b):
                dve.wait_ge(max_read, 2 * TB * (b + 1))
                t = slice(TB * b, TB * (b + 1))
                rows = nmax[:, t, :].rearrange("p t (g j) -> p t g j", g=G)
                link(dve.tensor_copy(nm_cols[:, t, :, 1:1 + GH], rows))
                dve.tensor_tensor(nm_cols[:, t, :, 1 + GH:1 + 2 * GH], rows, nm_cols[:, t, :, 1:1 + GH].bitcast(F32),
                                  ALU.subtract).then_inc(nm_ready, 1)

            def normed_values(b):
                dve.wait_ge(sums_ready, 2 * (b + 1))
                link(dve.reciprocal(sumT[:], sumT[:]))
                for gg in range(2):
                    dve.tensor_tensor(attnT[PV[gg], b % 2, :], bank[4 + b % 2][PV[gg], gg * S:(gg + 1) * S], sumT[PV[gg], :],
                                      ALU.mult).then_inc(attn_ready, 1)

            def residual(b):
                dve.wait_ge(proj_done, b + 1)
                dve.wait_ge(xb_ready, b // BH + 1)
                t = slice(TB * b, TB * (b + 1))
                dve.tensor_tensor(x1[:, t, :], bank[7][:, 0:TB * D].rearrange("p (t d) -> p t d", t=TB),
                                  xb[:, t, :], ALU.add).then_inc(x1_ready, 1)
                dve.wait_ge(x1_ready, b + 1)
                norm_stats(x1, mv2, TB * b, TB * (b + 1)).then_inc(var2, 1)

            def second_norm(b):
                dve.wait_ge(rstd2_ready, b + 1)
                for t in range(TB * b, TB * (b + 1)):
                    normalise(x2n, x1, mv2, rstd2, t).then_inc(x2n_ready, 1)

            def logits(h):
                t = slice(h * TH, (h + 1) * TH)
                dve.wait_ge(gate_done, BH * (h + 1))
                dve.wait_ge(ld_bg, 16)
                link(dve.tensor_tensor(logit[:, t, :], bank[x2_bank(BH * h)][:, S + h * TH * E:S + (h + 1) * TH * E].rearrange("p (t e) -> p t e", t=TH),
                                       bg_bc[:].unsqueeze(1).to_broadcast([P, TH, E]), ALU.add))
                link(dve.tensor_reduce(lmax[:, t], logit[:, t, :], AX.X, ALU.max))
                dve.tensor_tensor(logit[:, t, :], logit[:, t, :], lmax[:, t].unsqueeze(2).to_broadcast([P, TH, E]),
                                  ALU.subtract).then_inc(logit_ready, 1)

            def two_largest(h):
                t = slice(h * TH, (h + 1) * TH)
                bc = lambda a: a.to_broadcast([P, TH, E])
                dve.wait_ge(prob_exp, h + 1)
                link(dve.tensor_reduce(psumv[:, t], prob[:, t, :], AX.X, ALU.add))
                link(dve.reciprocal(psumv[:, t], psumv[:, t]))
                link(dve.tensor_tensor(prob[:, t, :], prob[:, t, :], bc(psumv[:, t].unsqueeze(2)), ALU.mult))
                for u in range(h * TH, (h + 1) * TH):
                    count(dve.max(top[:, u, :], prob[:, u, :]))
                dve.wait_ge(dve_step, steps[0])
                for u in range(h * TH, (h + 1) * TH):
                    count(dve.max_index(top_at[:, u, :], top[:, u, :], prob[:, u, :]))

            def select(h):
                t = slice(h * TH, (h + 1) * TH)
                bc = lambda a: a.to_broadcast([P, TH, E])
                dve.wait_ge(dve_step, steps[0])
                count(dve.tensor_tensor(first[:, t, :], col_e[:].unsqueeze(1).to_broadcast([P, TH, E]),
                                        bc(top_at[:, t, 0:1]), ALU.is_equal))
                count(dve.tensor_tensor(second[:, t, :], col_e[:].unsqueeze(1).to_broadcast([P, TH, E]),
                                        bc(top_at[:, t, 1:2]), ALU.is_equal))
                link(dve.tensor_tensor(norm[:, t], top[:, t, 0], top[:, t, 1], ALU.add))
                count(dve.tensor_tensor(first[:, t, :], first[:, t, :], second[:, t, :], ALU.add))
                link(dve.tensor_scalar(norm[:, t], norm[:, t], 1e-8, None, ALU.add))
                count(dve.reciprocal(norm[:, t], norm[:, t]))
                link(dve.tensor_tensor(sel[:, t, :], prob[:, t, :], first[:, t, :], ALU.mult))
                link(dve.tensor_tensor(sel[:, t, :], sel[:, t, :], bc(norm[:, t].unsqueeze(2)), ALU.mult))
                link(dve.tensor_copy(sel_parts[:, t, 0:E], sel[:, t, :]))
                dve.tensor_tensor(sel_parts[:, t, E:2 * E], sel[:, t, :], sel_parts[:, t, 0:E].bitcast(F32),
                                  ALU.subtract).then_inc(sel_ready, 1)

            q_lo_of(0, range(G))
            for t in range(TB):
                maxima(0, t)
            dve.wait_ge(fill_ready, 1)
            max_parts(0)
            first_norm(1)
            dve.wait_ge(v_done, 1)
            dve.wait_ge(ld_bv, 16)
            dve.wait_ge(v_filled, V_FILLS)
            for j in range(2):
                rows = slice(SK * j, SK * (j + 1))
                cols = slice(HD * j, HD * (j + 1))
                dve.tensor_tensor(v_diag[rows, :, :, cols],
                                  bank[5][rows, :].rearrange("p (b r w) -> p b r w", b=B, r=PR)[:, :, :, cols],
                                  bv_bc[rows, :].rearrange("p (r w) -> p r w", r=PR)[:, :, cols].unsqueeze(1)
                                  .to_broadcast([SK, B, PR, HD]), ALU.add).then_inc(v_ready, 1)
            dve.wait_ge(ident_ready, 1)
            dve.tensor_tensor(pick[:], ident[0:2 * E, 0:E], ident[0:2 * E, E:2 * E], ALU.add).then_inc(pick_ready, 1)
            for b in range(B):
                if b + 1 < B:
                    maxima(b + 1, 0)
                if b == 0:
                    dve.wait_ge(pick_ready, 1)
                    for e in range(2):
                        stage_b1(e, e)
                        stage_pick(e, e)
                if 2 <= b < B - 1:
                    second_norm(b - 2)
                if b + 1 < B:
                    maxima(b + 1, 1)
                    max_parts(b + 1)
                if b == 0:
                    q_lo_of(1, range(G))
                if b >= 1:
                    normed_values(b - 1)
                if b == B - 1:
                    second_norm(b - 2)
                if b >= 1:
                    residual(b - 1)
            logits(0)
            two_largest(0)
            second_norm(B - 2)
            normed_values(B - 1)
            residual(B - 1)

            def second_half(jj):
                if jj == 0:
                    second_norm(B - 1)
                if jj == 1:
                    select(0)
                if jj == 2:
                    logits(1)
                if jj == 6:
                    two_largest(1)
                if jj == 7:
                    select(1)

            def scale(i, uu):
                unit = 2 * NH * i + uu
                e = 2 * i + unit_of(uu)[0]
                r = uu % 2
                dve.wait_ge(down_done, HC * (unit + 1))
                dve.wait_ge(sel_copied, unit + 1)
                after(dve, y_added, unit - 1)
                bias = bias_cols[:, R2 + e:R2 + e + 1] if known(i) else bias_cols[:, bass.ds(R2 + e, 1)]
                dve.scalar_tensor_tensor(out=part[:, r, :], in0=bank[4 + r][:], scalar=bias, in1=sel_now[:, r, :],
                                         op0=ALU.add, op1=ALU.mult).then_inc(y_scaled, 1)

            def body(i):
                for jj in range(PER):
                    j = i * PER + jj
                    dve.wait_ge(gelu_done, j + 1)
                    dve.tensor_copy(hid_hi[:, jj % RING, :], hid[:, jj % RING, :]).then_inc(hid_split, 1)
                    if jj % HC < HC - 1 or last_chunk(i, jj):
                        dve.wait_ge(hid_split, j + 1)
                        hid_low(dve, jj).then_inc(lo_dve, 1)
                    if jj in SPLITS:
                        slot, which = SPLITS[jj]
                        e = 2 * i + 2 - slot
                        if not (known(i) and not 2 <= e < E):
                            last = PER * i + (0 if slot else 3 * HC)
                            dve.wait_ge((up_done, down_done)[which], last)
                            dve.tensor_copy(w_hi[:, slot, which, :], weight(e, which)).then_inc(wsplit_hi, 1)
                            if which == 0:
                                dve.wait_ge(gelu_done, last)
                                stage_b1(e, slot)
                            else:
                                stage_pick(e, slot)
                    if known(i) and i == 0:
                        second_half(jj)
                    if jj % HC == 0:
                        uu = jj // HC - 2
                        if uu >= 0:
                            scale(i, uu)
                        elif not known(i) or i > 0:
                            scale(i - 1, 2 * NH + uu)

            iterations(dve, body)
            scale(ITER - 1, 2 * NH - 2)
            scale(ITER - 1, 2 * NH - 1)
            for h in range(NH):
                dve.wait_ge(outT_done, h + 1)
                t = slice(h * TH, (h + 1) * TH)
                dve.tensor_tensor(y_out[:, t, :], bank[h][:].rearrange("p (t d) -> p t d", t=TH), x1[:, t, :],
                                  ALU.add).then_inc(out_ready, 1)

        @block.tensor
        def _(pe):
            pe.wait_ge(ident_ready, 1)

            def warm_up(n):
                for _ in range(n):
                    pe.transpose(bank[0][:, 0:P], ident[:], ident[:])

            warm_up(8)
            pe.wait_ge(ld_ctx, 16)
            for c in range(KEYS // P):
                ins = pe.transpose(bank[6][:, c * P:(c + 1) * P], ctx_sb[:, c, :], ident[:])
            ins.then_inc(ctxT_done, 1)
            warm_up(6)
            pe.wait_ge(ctxT_ready, 2)
            pe.wait_ge(rep_ready, 1)

            def keys(n):
                g = K_ORDER[n]
                pe.matmul(k_bank(g, 0, EXT), wk_rep[:, g, :, :].rearrange("p a c -> p (a c)"), ctxT[:, :, 0, :],
                          start=True, stop=True).then_inc(k_done, 1)

            keys(0)
            keys(1)
            pe.wait_ge(ld_bias, 16 * 4)
            pe.transpose(bank[5][:, 0:NR], bias_rows[:], ident[0:NR, 0:NR]).then_inc(biasT_done, 1)

            def turn_x(h):
                pe.wait_ge(xn_ready, TH * (h + 1))
                for t in range(TH):
                    ins = pe.transpose(bank[7 - h][:, t * P:(t + 1) * P], xn[:, h * TH + t, :], ident[:])
                ins.then_inc(xnT_done, 1)

            def queries(h, groups):
                pe.wait_ge(xnT_ready, h + 1)
                pe.wait_ge(rep_ready, 3)
                for g in groups:
                    if h == 0 and g >= 2:
                        pe.wait_ge(k_lo, G)
                    if h == 1 and g == 0:
                        pe.wait_ge(v_ready, 2)
                    if h == 1 and g >= 2:
                        pe.wait_ge(q_lo, G + g - 1)
                    pe.matmul(bank[Q_BANKS[h][g]][0:EXT + 1, :], wq_rep[:, g, :], xnT[:, h, :],
                              start=True, stop=True).then_inc(q_done, 1)

            def scores(b, n):
                t, half = TB * b + n // 2, n % 2
                at = 2 * TB * b + n
                if at >= 2:
                    pe.wait_ge(max_read, at - 1)
                for gg in range(2):
                    g = 2 * half + gg
                    ins = pe.matmul(bank[half][:, gg * 256:(gg + 1) * 256], q_st[0:EXT + 1, g, t * P:(t + 1) * P],
                                    k_blk[0:EXT + 1, g, b, :, :].rearrange("p j k -> p (j k)"), start=True, stop=True)
                ins.then_inc(s_done, 1)

            def max_rows(b):
                pe.wait_ge(nm_ready, b + 1)
                if b:
                    after(pe, x1_ready, b - 2)
                else:
                    pe.wait_ge(xnT_ready, 1)
                for t in range(TB):
                    ins = pe.transpose(bank[7][:, t * P:(t + 1) * P],
                                       nm_cols[:, TB * b + t, :, :].rearrange("p g r -> p (g r)").bitcast(F32), ident[:])
                ins.then_inc(nmT_done, 1)

            def scoresT(b, n):
                m = PR // 2 * b + n
                if st_bank(b, n) >= 2:
                    after(pe, exp_done, m - 1)
                else:
                    pe.wait_ge(max_read, 2 * T)
                for k in range(2):
                    pair = 2 * n + k
                    g, j = pair // 2, 2 * (pair % 2)
                    ins = pe.matmul(bank[st_bank(b, n)][:, k * S:(k + 1) * S], k_blk[:, g, b, j:j + 2, :].rearrange("p j k -> p (j k)"),
                                    q_st[:, g, b * S:(b + 1) * S], start=True, stop=True)
                ins.then_inc(st_done, 1)

            def values(b, gg, pairs=range(PR // 2)):
                if gg == 0 and 0 in pairs:
                    if b >= 2:
                        pe.wait_ge(attn_ready, 2 * (b - 1))
                    else:
                        pe.wait_ge(v_ready, 2)
                    if b == 1:
                        pe.wait_ge(q_lo, 2 * G)
                for pair in (PR // 2 * gg + p for p in pairs):
                    pe.wait_ge(exp_done, PR // 2 * b + pair // 2 + 1)
                    ins = pe.matmul(bank[4 + b % 2][:, gg * S:(gg + 1) * S], v_blk[:, b, pair * P:(pair + 1) * P],
                                    probsT[:, b % 2, pair, :], start=(pair % 4 == 0), stop=(pair % 4 == 3))
                if gg and PR // 2 - 1 in pairs:
                    ins.then_inc(pv_done, 1)

            def project(b):
                pe.wait_ge(attn_ready, 2 * (b + 1))
                pe.wait_ge(ld_wo, 16)
                pe.wait_ge(nmT_ready, G * min(b + 3, B))
                if b == B - 1:
                    pe.wait_ge(x2T_ready, b)
                for t in range(TB):
                    ins = pe.matmul(bank[7][:, t * D:(t + 1) * D], attnT[:, b % 2, t * P:(t + 1) * P], wo_sb[:],
                                    start=True, stop=True)
                ins.then_inc(proj_done, 1)

            def turn_x2(b):
                pe.wait_ge(x2n_ready, TB * (b + 1))
                if b:
                    pe.wait_ge(x2T_ready, b)
                    pe.wait_ge(x1_ready, b + 1)
                else:
                    pe.wait_ge(q_lo, 2 * G)
                for t in range(TB):
                    ins = pe.transpose(bank[x2_bank(b)][:, t * P:(t + 1) * P], x2n[:, TB * b + t, :], ident[:])
                ins.then_inc(x2T_done, 1)

            def gates(b):
                pe.wait_ge(x2T_ready, b + 1)
                pe.wait_ge(ld_wg, 16)
                for t in range(TB * b, TB * (b + 1)):
                    at = S + t * E
                    ins = pe.matmul(bank[x2_bank(b)][:, at:at + E], x2T[:, t * P:(t + 1) * P], wg_sb[:], start=True, stop=True)
                ins.then_inc(gate_done, 1)

            turn_x(0)
            keys(2)
            keys(3)
            queries(0, range(G))
            pe.wait_ge(bias_ready, 1)
            for b in range(B):
                ins = pe.matmul(bank[5][:, b * D:(b + 1) * D], ctxT[:, b, :, :].rearrange("p a k -> p (a k)"),
                                wkv_sb[:, D:2 * D], start=True, stop=True)
            ins.then_inc(v_done, 1)
            pe.wait_ge(q_lo, 2)
            pe.wait_ge(k_blk_dve, GH)
            pe.wait_ge(k_blk_pool, GH)
            pe.wait_ge(ext_ready, 1)
            pe.wait_ge(ext_copied, 16)
            scores(0, 0)
            pe.wait_ge(q_lo, G)
            pe.wait_ge(k_blk_act, 2 * GH)
            for n in range(1, 2 * TB):
                scores(0, n)
            pe.wait_ge(fill_ready, 1)
            max_rows(0)
            turn_x(1)
            for b in range(B):
                pe.wait_ge(nmT_ready, G * (b + 1))
                if b + 1 == BH:
                    pe.wait_ge(q_lo, 2 * G)
                for n in range(PR // 2):
                    scoresT(b, n)
                    if b + 1 < B:
                        scores(b + 1, n)
                if b == 0:
                    queries(1, (0, 1))
                if 2 <= b < B - 1:
                    turn_x2(b - 2)
                values(b, 0)
                if b == B - 1:
                    project(b - 1)
                    turn_x2(b - 2)
                if b + 1 < B:
                    max_rows(b + 1)
                if b == 0:
                    queries(1, (2, 3))
                if b == B - 1:
                    values(b, 1, range(0, 2))
                if b >= 2:
                    gates(b - 2)
                if b == B - 1:
                    values(b, 1, range(2, PR // 2))
                else:
                    values(b, 1)
                if 1 <= b < B - 1:
                    project(b - 1)

            def up(i, jj):
                j = i * PER + jj
                slot, c = unit_of(jj // HC)
                hc = jj % HC
                if hc == 0:
                    pe.wait_ge(wsplit, 2 * (2 * i + slot) + 1)
                if known(i) and i == 0 and jj in (0, 2 * HC):
                    pe.wait_ge(x2hi_ready, BH * (c + 1))
                    pe.wait_ge(x2lo_ready, BH * (c + 1))
                after(pe, gelu_done, j - RING + 1)
                w = slice(hc * P, (hc + 1) * P)
                q = slice(c * HT, (c + 1) * HT)
                for n, (a, m) in enumerate(((w_hi, x2T_hi), (w_hi, x2T_lo), (w_lo, x2T_hi))):
                    ins = pe.matmul(bank[jj % RING][:], a[:, slot, 0, w], m[:, q], start=(n == 0), stop=(n == 2))
                ins.then_inc(up_done, 1)

            def down(i, jj):
                j = i * PER + jj
                slot, c = unit_of(jj // HC)
                unit = 2 * NH * i + jj // HC
                hc = jj % HC
                if hc == 0:
                    pe.wait_ge(wsplit, 2 * (2 * i + slot) + 2)
                    after(pe, y_scaled, unit - 1)
                    if known(i) and i == 0 and jj == HC:
                        pe.wait_ge(attn_ready, 2 * B)
                if hc == HC - 1:
                    if known(i) and i == 0:
                        pe.wait_ge(selT_ready, c + 1)
                    after(pe, sel_copied, unit)
                    pe.wait_ge(staged, 2 * (2 * i + slot + 1))
                    pe.matmul(bank[6][:], pick_now[:, slot, :], selT[:, c, :], start=True, stop=True).then_inc(bc_done, 1)
                wait_lo(pe, i * 2 * NH + jj // HC, hc)
                w = slice(hc * D, (hc + 1) * D)
                for n, (a, m) in enumerate(((w_hi, hid_hi), (w_hi, hid_lo), (w_lo, hid_hi))):
                    ins = pe.matmul(bank[4 + jj // HC % 2][:], a[:, slot, 1, w], m[:, jj % RING, :],
                                    start=(hc == 0 and n == 0), stop=(hc == HC - 1 and n == 2))
                ins.then_inc(down_done, 1)

            def turn_sel(h):
                pe.wait_ge(sel_ready, h + 1)
                pe.wait_ge(logit_ready, h + 1)
                for t in range(TH):
                    ins = pe.transpose(bank[6 + h][0:2 * E, t * P:(t + 1) * P],
                                       sel_parts[:, h * TH + t, :].bitcast(F32), ident[:])
                ins.then_inc(selT_done, 1)

            pe.wait_ge(exp_done, PR // 2 * B)
            up(0, 0)
            turn_x2(B - 2)
            up(0, 1)
            gates(B - 2)
            up(0, 2)
            project(B - 1)
            up(0, 3)

            def turn_back(h, src, start, stop):
                for t in range(TH):
                    ins = pe.matmul(bank[h][:, t * P:(t + 1) * P], src[:, t * P:(t + 1) * P], ident[:],
                                    start=(start and t == 0), stop=(stop and t == TH - 1))
                return ins

            def body(i):
                for jj in range(PER):
                    if known(i) and i == 0:
                        if jj == 1:
                            turn_x2(B - 1)
                        if jj == 2:
                            gates(B - 1)
                            turn_sel(0)
                        if jj == 8:
                            turn_sel(1)
                    if last_chunk(i, jj):
                        pe.wait_ge(gelu_done, E * NH * HC)
                        pe.wait_ge(y_added, NH * E - 2)
                        turn_back(0, acc[:, 0, :], True, True).then_inc(outT_done, 1)
                    down(i, jj)
                    if jj + AHEAD < PER:
                        up(i, jj + AHEAD)
                    elif not known(i) or i < ITER - 1:
                        up(i + 1, jj + AHEAD - PER)

            iterations(pe, body)
            pe.wait_ge(y_added, NH * E - 1)
            turn_back(1, acc[:, 1, :], True, False)
            pe.wait_ge(y_scaled, NH * E)
            turn_back(1, part[:, 1, :], False, True).then_inc(outT_done, 1)

    return nc


INS = ["x", "ctx_1024", "mask_BxS2_bk0", "L0_xattn_Wq", "L0_xattn_bq", "L0_xattn_Wkv", "L0_xattn_bkv",
       "L0_xattn_Wo", "L0_xattn_bo", "L0_ffn_Wg", "L0_ffn_bg", "L0_ffn_W1", "L0_ffn_b1", "L0_ffn_W2", "L0_ffn_b2"]


def kernel(**inputs):
    import numpy as np
    import concourse.bacc as bacc
    from concourse.bass_utils import run_bass_kernel_spmd

    nc = bacc.Bacc("TRN2", target_bir_lowering=False, num_devices=1)
    arrays, args = {}, []
    for name in INS:
        a = np.ascontiguousarray(inputs[name])
        arrays[f"in_{name}"] = a
        args.append(nc.dram_tensor(f"in_{name}", a.shape, mybir.dt.from_np(a.dtype), kind="ExternalInput").ap())
    args.append(nc.dram_tensor("out_y", arrays["in_x"].shape, F32, kind="ExternalOutput").ap())
    build(nc, *args)
    r = run_bass_kernel_spmd(nc, [arrays], core_ids=[0])
    return r.results[0]["out_y"]
```
